# Optimizing a Trainium2 kernel written in Bass

```python
import numpy as np
import jax
import jax.numpy as jnp

def _softmax(x, axis=-1):
    return jax.nn.softmax(x, axis=axis)

def _gelu(x):
    return jax.nn.gelu(x, approximate=True)

def _silu(x):
    return jax.nn.silu(x)

def _sigmoid(x):
    return jax.nn.sigmoid(x)

def _layernorm(x, axis=-1, eps=1e-05):
    m = jnp.mean(x, axis=axis, keepdims=True)
    v = jnp.var(x, axis=axis, keepdims=True)
    return (x - m) / jnp.sqrt(v + eps)

def _scatter_add(tgt, idx, src, axis=0):
    return tgt.at[idx].add(src)

def _segment_sum(src, seg, n):
    return jax.ops.segment_sum(src, seg, n)
kernel_name = 'mk_seq_postln_d1_jaxref_r4_505b35'

def setup_inputs(seed: int=0):
    np.random.seed(seed)
    _w = jnp.asarray

    def _L0_attn_setup():
        import jax, jax.numpy as jnp
        import numpy as np
        HIDDEN = 512
        HEADS = 16
        HEAD_DIM = HIDDEN // HEADS
        NEG = -10000000000.0
        key = jax.random.key(seed)
        k1, k2, k3 = jax.random.split(key, 3)
        x = jax.random.normal(k1, (2, 512, HIDDEN), dtype=jnp.float32)
        w_qkv = jax.random.normal(k2, (HIDDEN, 3 * HIDDEN), dtype=jnp.float32) / np.sqrt(HIDDEN)
        w_out = jax.random.normal(k3, (HIDDEN, HIDDEN), dtype=jnp.float32) / np.sqrt(HIDDEN)
        return {'x': x, 'w_qkv': w_qkv, 'w_out': w_out}
    _L0_attn_in = _L0_attn_setup()

    def _L0_ffn_setup():
        import jax, jax.numpy as jnp
        import numpy as np
        B, S, D = (2, 512, 512)
        I = 256
        E = 32
        K = 4
        NS = 1
        ALPHA = 7.0

        def _clamped_swiglu(x, wg, wu, wd):
            g = jnp.clip(x @ wg.T, -ALPHA, ALPHA)
            u = jnp.clip(x @ wu.T, -ALPHA, ALPHA)
            return jax.nn.silu(g) * u @ wd.T
        key = jax.random.key(seed)
        ks = jax.random.split(key, 9)
        s = 0.02
        return {'hidden': jax.random.normal(ks[0], (B, S, D), jnp.float32), 'router_w': jax.random.normal(ks[1], (E, D), jnp.float32) * s, 'expert_bias': jax.random.normal(ks[2], (E,), jnp.float32) * s, 'gate_w': jax.random.normal(ks[3], (E, I, D), jnp.float32) * s, 'up_w': jax.random.normal(ks[4], (E, I, D), jnp.float32) * s, 'down_w': jax.random.normal(ks[5], (E, D, I), jnp.float32) * s, 'shared_gate_w': jax.random.normal(ks[6], (NS * I, D), jnp.float32) * s, 'shared_up_w': jax.random.normal(ks[7], (NS * I, D), jnp.float32) * s, 'shared_down_w': jax.random.normal(ks[8], (D, NS * I), jnp.float32) * s}
    _L0_ffn_in = _L0_ffn_setup()
    _d = {'L0_attn_x': _L0_attn_in['x'], 'L0_attn_w_qkv': _L0_attn_in['w_qkv'], 'L0_attn_w_out': _L0_attn_in['w_out'], 'L0_ffn_router_w': _L0_ffn_in['router_w'], 'L0_ffn_expert_bias': _L0_ffn_in['expert_bias'], 'L0_ffn_gate_w': _L0_ffn_in['gate_w'], 'L0_ffn_up_w': _L0_ffn_in['up_w'], 'L0_ffn_down_w': _L0_ffn_in['down_w'], 'L0_ffn_shared_gate_w': _L0_ffn_in['shared_gate_w'], 'L0_ffn_shared_up_w': _L0_ffn_in['shared_up_w'], 'L0_ffn_shared_down_w': _L0_ffn_in['shared_down_w']}
    _x0 = _d['L0_attn_x']
    _d['L0_attn_x'] = jax.random.normal(jax.random.fold_in(jax.random.key(seed), 1), (2, 1024, 512), dtype=_x0.dtype)
    del _x0
    return _d

def reference(L0_attn_x, L0_attn_w_qkv, L0_attn_w_out, L0_ffn_router_w, L0_ffn_expert_bias, L0_ffn_gate_w, L0_ffn_up_w, L0_ffn_down_w, L0_ffn_shared_gate_w, L0_ffn_shared_up_w, L0_ffn_shared_down_w):

    def _L0_attn_ref(x, w_qkv, w_out):
        import jax, jax.numpy as jnp
        import numpy as np
        HIDDEN = 512
        HEADS = 16
        HEAD_DIM = HIDDEN // HEADS
        NEG = -10000000000.0
        b, s, _ = x.shape
        qkv = x @ w_qkv
        qkv = qkv.reshape(b, s, 3, HEADS, HEAD_DIM)
        q, k, v = (qkv[:, :, 0], qkv[:, :, 1], qkv[:, :, 2])
        scale = jnp.sqrt(jnp.float32(HEAD_DIM)).astype(x.dtype)
        q = q / scale
        scores = jnp.einsum('bqhd,bkhd->bhqk', q, k)
        causal_mask = jnp.arange(s)[:, None] >= jnp.arange(s)[None, :]
        scores = jnp.where(causal_mask[None, None], scores, NEG)
        attn = jax.nn.softmax(scores, axis=-1)
        out = jnp.einsum('bhqk,bkhd->bqhd', attn, v).reshape(b, s, HIDDEN)
        return out @ w_out

    def _L0_ffn_ref(hidden, router_w, expert_bias, gate_w, up_w, down_w, shared_gate_w, shared_up_w, shared_down_w):
        import jax, jax.numpy as jnp
        import numpy as np
        B, S, D = (2, 512, 512)
        I = 256
        E = 32
        K = 4
        NS = 1
        ALPHA = 7.0

        def _clamped_swiglu(x, wg, wu, wd):
            g = jnp.clip(x @ wg.T, -ALPHA, ALPHA)
            u = jnp.clip(x @ wu.T, -ALPHA, ALPHA)
            return jax.nn.silu(g) * u @ wd.T
        Bb, Ss, Dd = hidden.shape
        flat = hidden.reshape(-1, Dd)
        T = flat.shape[0]
        logits = flat @ router_w.T
        scores = jnp.sqrt(jax.nn.softplus(logits))
        _, idx = jax.lax.top_k(scores + expert_bias, K)
        topv = jnp.take_along_axis(scores, idx, axis=1)
        topv = topv / (topv.sum(axis=-1, keepdims=True) + 1e-20)
        probs = jnp.zeros((T, E), flat.dtype).at[jnp.arange(T)[:, None], idx].set(topv)

        def body(acc, xs):
            wg, wu, wd, p = xs
            return (acc + p[:, None] * _clamped_swiglu(flat, wg, wu, wd), None)
        out, _ = jax.lax.scan(body, jnp.zeros_like(flat), (gate_w, up_w, down_w, probs.T))
        out = out + _clamped_swiglu(flat, shared_gate_w, shared_up_w, shared_down_w)
        return out.reshape(Bb, Ss, Dd)
    x = L0_attn_x
    x = _layernorm(x + _L0_attn_ref(x, L0_attn_w_qkv, L0_attn_w_out), axis=-1)
    x = _layernorm(x + _L0_ffn_ref(x, L0_ffn_router_w, L0_ffn_expert_bias, L0_ffn_gate_w, L0_ffn_up_w, L0_ffn_down_w, L0_ffn_shared_gate_w, L0_ffn_shared_up_w, L0_ffn_shared_down_w), axis=-1)
    return x

_drawn_inputs = setup_inputs


def setup_inputs(seed=0):
    import zlib

    import numpy as np

    out = dict(_drawn_inputs(seed))
    spreads = {}
    factors = {'L0_ffn_router_w': 3.487,
     'L0_ffn_expert_bias': 8.0,
     'L0_ffn_gate_w': 3.308,
     'L0_ffn_up_w': 3.242,
     'L0_ffn_down_w': 3.239}
    for name, (base, spread) in spreads.items():
        noise = np.random.default_rng([zlib.crc32(name.encode()), seed]).standard_normal(out[name].shape)
        drawn = base * np.exp(spread * noise) if base else spread * noise
        out[name] = jnp.asarray(drawn.astype(out[name].dtype))
    for name, factor in factors.items():
        out[name] = (out[name] * factor).astype(out[name].dtype)
    return out
```

```python
import itertools
from contextlib import ExitStack

import numpy as np

import concourse.bass as bass
from concourse import mybir

F32 = mybir.dt.float32
F32R = mybir.dt.float32r
BF16 = mybir.dt.bfloat16
I32 = mybir.dt.int32
U32 = mybir.dt.uint32
ALU = mybir.AluOpType
ACT = mybir.ActivationFunctionType
AX = mybir.AxisListType

P = 128
B, S, D = 2, 1024, 512
H, HD = 16, 32
E, I, TOPK = 32, 256, 4
T = B * S
NT = T // P
DC = D // P
IC = I // P
NH = B * H
G = 512
NG = T // G
KB = S // P
WCOLS = DC * 2 * I + IC * D
DOWN0 = DC * 2 * I
TILES_MAX = NT + T * TOPK // P + E
ALPHA = 7.0
EPS = 1e-5
NEG = -1e30
INV_SQRT_HD = float(1.0 / np.sqrt(np.float32(HD)))

CHUNKS = [
    dict(group=1, st=[(0, 512, 512, 0), (1, 512, 512, 512)], cols=1024,
         pv=[(0, 0, 512, 0), (1, 512, 512, 0)], diag=None),
    dict(group=1, st=[(2, 512, 512, 0), (3, 512, 512, 512)], cols=1024,
         pv=[(2, 0, 512, 0), (3, 512, 512, 0)], diag=None),
    dict(group=1, st=[(4, 512, 512, 0), (5, 640, 384, 512)], cols=896,
         pv=[(4, 0, 512, 0), (5, 512, 384, 128)], diag=512),
    dict(group=1, st=[(6, 768, 256, 0), (7, 768, 256, 256)], cols=512,
         pv=[(6, 0, 256, 256), (7, 384, 128, 384)], diag=384),
    dict(group=0, st=[(0, 0, 512, 0), (1, 128, 384, 512)], cols=896,
         pv=[(0, 0, 512, 0), (1, 512, 384, 128)], diag=512),
    dict(group=0, st=[(2, 256, 256, 0), (3, 256, 256, 256)], cols=512,
         pv=[(2, 0, 256, 256), (3, 384, 128, 384)], diag=384),
]
NC_ = len(CHUNKS)
PIECES = [(t, 0, (t + 1) * P, True) for t in range(4)]
for _t in range(4, 8):
    PIECES += [(_t, 0, 512, False), (_t, 512, (_t - 3) * P, True)]
NP_ = len(PIECES)
SEQ = NP_ + 1


class Mem:

    def __init__(self, nc, ctx):
        self.nc, self.ctx = nc, ctx

    def sb(self, name, shape, dt=F32):
        return self.ctx.enter_context(self.nc.sbuf_tensor(name, shape, dt))

    def ps(self, name, shape, dt=F32):
        return self.ctx.enter_context(self.nc.psum_tensor(name, shape, dt))

    def sem(self, name):
        return self.ctx.enter_context(self.nc.semaphore(name))


def value(eng, n):
    return n if isinstance(n, int) else eng.to_reg(n)


def f32(ap):
    return ap.bitcast(F32)


def product(pe, out, pairs):
    for n, (l, r) in enumerate(pairs):
        mm = pe.matmul(out, l, r, start=(n == 0), stop=(n == len(pairs) - 1))
    return mm


def split3(lh, ll, rh, rl):
    return [(lh, rh), (lh, rl), (ll, rh)]


def project(nc, xT, w_qkv, q_hi, q_lo, k_hi, k_lo, v_all):
    with ExitStack() as ctx:
        m = Mem(nc, ctx)
        w_raw = m.sb("w_raw", [P, DC, 3 * D])
        w_hi = m.sb("w_hi", [P, DC, 3 * D], F32R)
        w_lo = m.sb("w_lo", [P, DC, 3 * D], F32R)
        x_raw = m.sb("x_raw", [P, NG, DC, G])
        x_hi = m.sb("x_hi", [P, 2, DC, G], F32R)
        x_lo = m.sb("x_lo", [P, 2, DC, G], F32R)
        out_hi = m.sb("out_hi", [P, 4, G], F32R)
        out_lo = m.sb("out_lo", [P, 4, G], F32R)
        acc = m.ps("acc_qkv", [P, 4, G])
        w_in = [m.sem(f"w_in{n}") for n in range(3)]
        x_in = [m.sem(f"x_in{s}") for s in range(2)]
        w_high, w_low = m.sem("w_high"), m.sem("w_low")
        x_high, x_low = m.sem("x_high"), m.sem("x_low")
        made = m.sem("made")
        high = m.sem("high")
        low = m.sem("low")
        stored = [m.sem(f"stored{n}") for n in range(4)]
        block = ctx.enter_context(nc.Block("project"))
        NO = 12

        xT_v = xT.rearrange("(c p) t -> p c t", p=P)
        w_v = w_qkv.rearrange("(c p) n -> p c n", p=P)

        @block.sync
        def _(sp):
            for n in range(4):
                sp.sem_inc(stored[n], 32)
            for n in range(3):
                sp.dma_start(w_raw[:, :, n * D:(n + 1) * D], w_v[:, :, n * D:(n + 1) * D]).then_inc(w_in[n], 16)
                if n == 0:
                    for s in range(2):
                        sp.dma_start(x_raw[:, s], xT_v[:, :, s * G:(s + 1) * G]).then_inc(x_in[s], 16)
            for s in range(2):
                sp.wait_ge(x_in[s], 16)
                sp.dma_start(x_raw[:, 2 + s], xT_v[:, :, (2 + s) * G:(3 + s) * G]).then_inc(x_in[s], 16)
            with sp.Fori(0, B) as b:
                for s in range(2):
                    for o in range(8):
                        hi_d, lo_d = (q_hi, q_lo) if o < 4 else (k_hi, k_lo)
                        n = 8 * (2 * b + s) + o + 1
                        rows = bass.ds(b * D + (o % 4) * P, P)
                        sp.wait_ge(high, n)
                        sp.dma_start(hi_d[rows, s * G:(s + 1) * G], f32(out_hi[:, o % 4])).then_inc(stored[o % 4], 16)
                        sp.wait_ge(low, 4 + NO * (2 * b + s) + o + 1)
                        sp.dma_start(lo_d[rows, s * G:(s + 1) * G], f32(out_lo[:, o % 4])).then_inc(stored[o % 4], 16)
            for n in range(4):
                sp.wait_ge(stored[n], 32 * (2 * NG + 1))

        @block.scalar
        def _(act):
            def weights(n):
                act.wait_ge(w_in[n], 16)
                act.activation(w_hi[:, :, n * D:(n + 1) * D], w_raw[:, :, n * D:(n + 1) * D], ACT.Copy).then_inc(w_high, 1)

            for n in range(3):
                weights(n)
            with act.Fori(0, B) as b:
                for s in range(2):
                    g = 2 * b + s
                    act.wait_ge(x_in[s], 16 * b + 16)
                    act.wait_ge(made, NO * (g + 1))
                    act.activation(x_hi[:, s:s + 1], x_raw[:, bass.ds(g, 1)], ACT.Copy).then_inc(x_high, 1)
                    for o in range(8):
                        act.wait_ge(made, 2 * NO + NO * g + o + 1)
                        act.wait_ge(stored[o % 4], 32 * (2 * g + o // 4 + 1))
                        act.activation(out_hi[:, o % 4], acc[:, o % 4], ACT.Copy,
                                       scale=INV_SQRT_HD if o < 4 else 1.0).then_inc(high, 1)

        @block.vector
        def _(dve):
            dve.sem_inc(low, 4)

            def weights(n):
                part = slice(n * D, (n + 1) * D)
                dve.wait_ge(w_high, n + 1)
                dve.tensor_tensor(w_lo[:, :, part], w_raw[:, :, part], f32(w_hi[:, :, part]), ALU.subtract).then_inc(w_low, 1)

            for n in range(3):
                weights(n)
            with dve.Fori(0, B) as b:
                for s in range(2):
                    g = 2 * b + s
                    dve.wait_ge(x_high, g + 1)
                    dve.tensor_tensor(x_lo[:, s:s + 1], x_raw[:, bass.ds(g, 1)], f32(x_hi[:, s:s + 1]), ALU.subtract).then_inc(x_low, 1)
                    for o in range(8):
                        dve.wait_ge(high, 8 * g + o + 1)
                        dve.wait_ge(stored[o % 4], 32 * (2 * g + o // 4 + 1))
                        dve.scalar_tensor_tensor(out_lo[:, o % 4], acc[:, o % 4], INV_SQRT_HD if o < 4 else 1.0,
                                                 f32(out_hi[:, o % 4]), ALU.mult, ALU.subtract).then_inc(low, 1)
                    for t in range(4):
                        dve.wait_ge(made, 2 * NO + NO * g + 8 + t + 1)
                        dve.tensor_copy(v_all[:, 4 * s + t, bass.ds(b * H, H), :],
                                        acc[:, t].rearrange("p (h d) -> p h d", d=HD)).then_inc(low, 1)

        @block.tensor
        def _(pe):
            pe.sem_inc(made, 2 * NO)
            with pe.Fori(0, B) as b:
                for s in range(2):
                    g = 2 * b + s
                    pe.wait_ge(x_low, g + 1)
                    for o in range(12):
                        pe.wait_ge(low, NO * g + o + 1)
                        if o % 4 == 0:
                            pe.wait_ge(w_low, o // 4 + 1)
                        pairs = []
                        for c in range(DC):
                            if o < 8:
                                col = slice((o // 4) * D + (o % 4) * P, (o // 4) * D + (o % 4 + 1) * P)
                                pairs += split3(w_hi[:, c, col], w_lo[:, c, col], x_hi[:, s, c], x_lo[:, s, c])
                            else:
                                tok = slice((o - 8) * P, (o - 7) * P)
                                pairs += split3(x_hi[:, s, c, tok], x_lo[:, s, c, tok],
                                                w_hi[:, c, 2 * D:], w_lo[:, c, 2 * D:])
                        product(pe, acc[:, o % 4], pairs).then_inc(made, 1)


def attend(nc, q_hi, q_lo, k_hi, k_lo, v_all, attn_T, den, xs_zero):
    with ExitStack() as ctx:
        m = Mem(nc, ctx)
        SETUP = 13
        RING = 4
        qs = [m.sb(f"qs{r}", [3 * HD + 1, S], F32R) for r in range(RING)]
        ks = [m.sb(f"ks{r}", [3 * HD + 1, S], F32R) for r in range(RING)]
        vs = [m.sb(f"vs{p}", [P, KB, 2 * HD]) for p in range(2)]
        mask = m.sb("mask", [P, 512])
        mx = [m.sb(f"mx{p}", [P, KB]) for p in range(2)]
        mx2 = [m.sb(f"mx2{p}", [P, 8]) for p in range(2)]
        neg_row = [m.sb(f"neg_row{r}", [KB, P], F32R) for r in range(RING)]
        ident = m.sb("ident_a", [P, P])
        probs = [m.sb(f"probs{r}", [P, 1024]) for r in range(3)]
        o_sb = [[m.sb(f"o{p}{g}", [HD + 1, 512]) for g in range(2)] for p in range(2)]
        zeros = m.sb("zeros", [P, D])
        ps_st = [m.ps(f"ps_st{r}", [P, 1024]) for r in range(2)]
        ps_s = [m.ps(f"ps_s{r}", [P, 512]) for r in range(2)]
        ps_o = [m.ps(f"ps_o{g}", [P, 512]) for g in range(2)]

        loaded = [m.sem(f"loaded{r}") for r in range(RING)]
        row_in = [m.sem(f"row_in{r}") for r in range(RING)]
        st_done = m.sem("st_done")
        s_done = m.sem("s_done")
        pv_done = m.sem("pv_done")
        exp_done = m.sem("exp_done")
        row_done = m.sem("row_done")
        masked = m.sem("masked")
        v_done = m.sem("v_done")
        s_taken = m.sem("s_taken")
        max_done = m.sem("max_done")
        o_done = m.sem("o_done")
        o_out = [[m.sem(f"o_out{p}{g}") for g in range(2)] for p in range(2)]
        setup = m.sem("setup")
        zeroed = [m.sem(f"zeroed{p}") for p in range(2)]
        block = ctx.enter_context(nc.Block("attend"))

        def load(sp, i, r):
            rows = bass.ds(i * HD, HD)
            for n, (qd, kd) in enumerate(((q_hi, k_hi), (q_hi, k_lo), (q_lo, k_hi))):
                sp.dma_start(f32(qs[r][n * HD:(n + 1) * HD, :]), qd[rows, :]).then_inc(loaded[r], 16)
                sp.dma_start(f32(ks[r][n * HD:(n + 1) * HD, :]), kd[rows, :]).then_inc(loaded[r], 16)

        @block.sync
        def _(sp):
            for r in range(RING):
                sp.sem_inc(row_in[r], 16)
            for p in range(2):
                for g in range(2):
                    sp.sem_inc(o_out[p][g], 32)
                sp.sem_inc(zeroed[p], 16)

            def send_row(j, r):
                sp.wait_ge(row_done, RING * j + (r + 1))
                sp.dma_start(f32(qs[r % RING][3 * HD:3 * HD + 1, :].rearrange("o (t x) -> o t x", x=P)),
                             f32(neg_row[r % RING][:, :])).then_inc(row_in[r % RING], 16)

            def store(i, p, g):
                cols = slice(g * 512, (g + 1) * 512)
                count = value(sp, 2 + 2 * i + (1 if g == 1 else 2))
                sp.wait_ge(loaded[p], 96)
                sp.wait_ge(o_done, count)
                sp.dma_start(attn_T[bass.ds(i * HD, HD), cols], o_sb[p][g][0:HD, :]).then_inc(o_out[p][g], 16)
                sp.dma_start(den[bass.ds(i, 1), cols], o_sb[p][g][HD:HD + 1, :]).then_inc(o_out[p][g], 16)

            def zero(i, p):
                rows = (TILES_MAX - NT) * P // NH
                sp.dma_start(xs_zero[bass.ds(i * rows, rows), :].rearrange("(n q) d -> q n d", q=P),
                             zeros[:].rearrange("q (o d) -> q o d", o=1).to_broadcast([P, rows // P, D])).then_inc(zeroed[p], 16)

            def head(j, r):
                i, p = RING * j + r, r % 2
                static = isinstance(j, int)
                if not static:
                    sp.wait_ge(st_done, NC_ * (i + 1))
                    load(sp, i + RING, r)
                for g in (1, 0):
                    store(i, p, g)
                if not static or r + 2 < RING:
                    send_row(j, r + 2)
                sp.wait_ge(zeroed[p], 16 * (2 * j + r // 2) + 16)
                zero(i, p)

            for r in range(RING):
                load(sp, r, r)
            for r in range(2):
                send_row(0, r)
            with sp.Fori(0, NH // RING - 1) as j:
                for r in range(RING):
                    head(j, r)
            for r in range(RING):
                head(NH // RING - 1, r)
            for p in range(2):
                for g in range(2):
                    sp.wait_ge(o_out[p][g], 32 * (NH // 2 + 1))
                sp.wait_ge(zeroed[p], 16 * (NH // 2 + 1))

        @block.gpsimd
        def _(pool):
            pool.memset(zeros[:], 0.0).then_inc(setup, 1)
            pool.memset(ident[:], 0.0).then_inc(setup, 1)
            pool.memset(mask[:], 0.0).then_inc(setup, 1)
            for p in range(2):
                pool.memset(vs[p][:, :, HD:], 1.0).then_inc(setup, 1)
            pool.wait_ge(setup, 5)
            pool.affine_select(out=ident[:], in_=ident[:], compare_op=ALU.not_equal, fill=1.0, base=0,
                               pattern=[[-1, P]], channel_multiplier=1).then_inc(setup, 1)
            pool.affine_select(out=mask[:, 384:], in_=mask[:, 384:], compare_op=ALU.is_ge, fill=NEG, base=0,
                               pattern=[[-1, P]], channel_multiplier=1).then_inc(setup, 1)

            def values(i, p):
                if not isinstance(i, int) or i >= 2:
                    pool.wait_ge(pv_done, 12 + NC_ * (i - 1))
                pool.tensor_copy(vs[p][:, :, 0:HD].rearrange("p k (o d) -> p k o d", o=1),
                                 v_all[:, :, bass.ds(i, 1), :]).then_inc(v_done, 1)

            def masks(i):
                for k in range(2, NC_):
                    gap = CHUNKS[k]["diag"]
                    count = value(pool, 2 + NC_ * i + k + 1)
                    pool.wait_ge(setup, SETUP)
                    pool.wait_ge(exp_done, count)
                    at = probs[k % 3][:, 0:2 * gap].rearrange("p (a x) -> p a x", a=2)[:, :, 0:P]
                    pool.affine_select(out=at, in_=at, compare_op=ALU.is_ge, fill=0.0, base=0,
                                       pattern=[[0, 2], [1, P]], channel_multiplier=-1).then_inc(masked, 1)

            values(0, 0)
            with pool.Fori(0, NH // 2 - 1) as j:
                for p in range(2):
                    values(2 * j + (p + 1), 1 - p)
                    masks(2 * j + p)
            values(NH - 1, 1)
            masks(NH - 2)
            masks(NH - 1)

        @block.scalar
        def _(act):
            act.sem_inc(exp_done, 2)

            def row(j, r):
                slot = (SEQ * (r % 2) + NP_) % 2
                act.wait_ge(s_done, SEQ * (RING * j + r) + SEQ)
                act.wait_ge(row_in[r % RING], 16 * (j + r // RING) + 16)
                act.activation(neg_row[r % RING][:, :], ps_s[slot][0:KB, 0:P], ACT.Copy, scale=-1.0).then_inc(row_done, 1)

            def head(j, r):
                i = RING * j + r
                if not (isinstance(i, int) and i == NH - 1):
                    row(j, r + 1)
                for k in range(NC_):
                    n = CHUNKS[k]["cols"]
                    act.wait_ge(st_done, NC_ * i + k + 1)
                    act.wait_ge(pv_done, NC_ * i + k + 10)
                    act.activation(probs[k % 3][:, 0:n], ps_st[k % 2][:, 0:n], ACT.Exp).then_inc(exp_done, 1)

            row(0, 0)
            with act.Fori(0, NH // RING - 1) as j:
                for r in range(RING):
                    head(j, r)
            for r in range(RING):
                head(NH // RING - 1, r)

        @block.vector
        def _(dve):
            dve.sem_inc(o_done, 2)
            dve.wait_ge(setup, 7)
            for r in range(RING):
                dve.memset(f32(ks[r][3 * HD:3 * HD + 1, :]), 1.0).then_inc(setup, 1)
            for p in range(2):
                dve.memset(mx2[p][:], NEG).then_inc(setup, 1)

            def maxima(i, p, q0, q1):
                for q in range(q0, q1):
                    t, k0, w, diag = PIECES[q]
                    bank = ps_s[(SEQ * p + q) % 2][:, 0:w]
                    out = mx[p][:, t:t + 1] if t < 4 or not diag else mx2[p][:, t:t + 1]
                    count = value(dve, SEQ * i + q + 1)
                    if diag:
                        dve.wait_ge(setup, SETUP)
                    dve.wait_ge(s_done, count)
                    if diag:
                        dve.tensor_tensor_reduce(bank, bank, mask[:, 512 - w:], 1.0, -3e38, ALU.add, ALU.max,
                                                 out).then_inc(s_taken, 1)
                    else:
                        dve.tensor_reduce(out, bank, AX.X, ALU.max).then_inc(s_taken, 1)
                if q1 == NP_:
                    dve.wait_ge(s_taken, NP_ * (i + 1))
                    dve.tensor_tensor(mx[p][:, 4:8], mx[p][:, 4:8], mx2[p][:, 4:8], ALU.max).then_inc(max_done, 1)

            def output(j, r, g):
                p = r % 2
                dve.wait_ge(o_out[p][g], 32 * (2 * j + r // 2) + 32)
                dve.wait_ge(pv_done, 12 + NC_ * (RING * j + r) + (4 if g == 1 else 6))
                dve.tensor_copy(o_sb[p][g][:, :], ps_o[g][0:HD + 1, :]).then_inc(o_done, 1)

            def head(j, r, ahead):
                if ahead:
                    maxima(RING * j + (r + 2), r % 2, 0, 10)
                output(j, r, 1)
                if ahead:
                    maxima(RING * j + (r + 2), r % 2, 10, NP_)
                output(j, r, 0)

            for i in range(2):
                maxima(i, i, 0, NP_)
            with dve.Fori(0, NH // RING - 1) as j:
                for r in range(RING):
                    head(j, r, True)
            for r in range(RING):
                head(NH // RING - 1, r, r + 2 < RING)

        @block.tensor
        def _(pe):
            def piece(j, r, q):
                i, p = RING * j + r, r % 2
                first = isinstance(i, int) and i == 0
                t, k0, w, _ = PIECES[q]
                w = max(w, 2 * P)
                if q == 0:
                    pe.wait_ge(loaded[r % RING], 96 * (j + r // RING) + 96)
                    if not first:
                        pe.wait_ge(s_taken, NP_ * i)
                elif q == 1:
                    if not first:
                        pe.wait_ge(row_done, i)
                else:
                    pe.wait_ge(s_taken, NP_ * i + q - 1)
                pe.matmul(ps_s[(SEQ * p + q) % 2][:, 0:w], qs[r % RING][0:3 * HD, t * P:(t + 1) * P],
                          ks[r % RING][0:3 * HD, k0:k0 + w], start=True, stop=True).then_inc(s_done, 1)

            def turn(j, r):
                p = r % 2
                pe.wait_ge(max_done, RING * j + (r + 1))
                pe.transpose(ps_s[(SEQ * p + NP_) % 2][0:KB, 0:P], mx[p][:, :], ident[:]).then_inc(s_done, 1)

            def scores_T(j, r, k):
                if k == 0:
                    pe.wait_ge(row_in[r], 16 * j + 32)
                pe.wait_ge(exp_done, NC_ * (RING * j + r) + k + 1)
                for kb, q0, w, col in CHUNKS[k]["st"]:
                    mm = pe.matmul(ps_st[k % 2][:, col:col + w], ks[r][:, kb * P:(kb + 1) * P],
                                   qs[r][:, q0:q0 + w], start=True, stop=True)
                mm.then_inc(st_done, 1)

            def values(j, r, k):
                i, p = RING * j + r, r % 2
                g = CHUNKS[k]["group"]
                if k == 0:
                    pe.wait_ge(v_done, i + 1)
                    pe.wait_ge(o_done, 2 * i + 1)
                if k == 4:
                    pe.wait_ge(o_done, 2 * i + 2)
                if k < 2:
                    pe.wait_ge(exp_done, 2 + NC_ * i + k + 1)
                else:
                    pe.wait_ge(masked, 4 * i + k - 1)
                pv = CHUNKS[k]["pv"]
                for n, (kb, col, w, q0) in enumerate(pv):
                    mm = pe.matmul(ps_o[g][0:2 * HD, q0:q0 + w], vs[p][:, kb, :], probs[k % 3][:, col:col + w],
                                   start=(kb == 0), stop=(k in (3, 5) and n == 1), skip_group_check=True)
                mm.then_inc(pv_done, 1)

            def head(j, r, turning, ahead):
                for k in range(NC_):
                    if k == 0 and turning:
                        turn(j, r + 1)
                    if ahead:
                        piece(j, r + 2, 2 * k)
                    scores_T(j, r, k)
                    if ahead:
                        piece(j, r + 2, 2 * k + 1)
                    if k > 0:
                        values(j, r, k - 1)
                values(j, r, NC_ - 1)

            pe.sem_inc(pv_done, 12)
            pe.wait_ge(setup, SETUP)
            for q in range(NP_):
                piece(0, 0, q)
            turn(0, 0)
            for q in range(NP_):
                piece(0, 1, q)
            with pe.Fori(0, NH // RING - 1) as j:
                for r in range(RING):
                    head(j, r, True, True)
            for r in range(RING):
                head(NH // RING - 1, r, r + 1 < RING, r + 2 < RING)


def mix(nc, attn_T, den, rden, w_out, x, router_wT, ident, x1_all, logits):
    with ExitStack() as ctx:
        m = Mem(nc, ctx)
        SUB = S // G
        TB = S // P
        TG = G // P
        LAG = 2
        STEPS = 5
        den_sb = m.sb("den_sb", [P, NH * S // P])
        w_raw = m.sb("wo_raw", [P, DC, D])
        w_hi = m.sb("wo_hi", [P, DC, D], F32R)
        w_lo = m.sb("wo_lo", [P, DC, D], F32R)
        r_raw = m.sb("rw_raw", [P, DC, E])
        r_hi = m.sb("rw_hi", [P, DC, P], F32R)
        r_lo = m.sb("rw_lo", [P, DC, P], F32R)
        a_n = [m.sb(f"a_n{s}", [P, DC, G]) for s in range(SUB)]
        a_rd = [m.sb(f"a_rd{s}", [P, DC, G]) for s in range(SUB)]
        a_hi = [m.sb(f"a_hi{s}", [P, DC, G], F32R) for s in range(SUB)]
        a_lo = [m.sb(f"a_lo{s}", [P, DC, G], F32R) for s in range(SUB)]
        x_nat = [m.sb(f"x_nat{s}", [P, TG, D]) for s in range(SUB)]
        x1 = m.sb("x1_new", [P, 4, D])
        xT_hi = m.sb("x1T_hi", [P, DC, G], F32R)
        xT_lo = m.sb("x1T_lo", [P, DC, G], F32R)
        lgT = m.sb("lgT", [E, G])
        stats = m.sb("stats1", [P, 4, 6])
        mv = m.sb("mv1", [P, 4, 2])
        std = m.sb("std1", [P, 4, 1])
        rstd = m.sb("rstd1", [P, 4, 1])
        eps = m.sb("eps1", [P, 1])
        ps_y = m.ps("ps_y", [P, 4, D])
        ps_t = m.ps("ps_t", [P, 2, D])
        ps_lT = m.ps("ps_lT", [P, G])
        ps_l = m.ps("ps_l", [P, TG, P])

        den_in, den_out, w_in, r_in = m.sem("den_in"), m.sem("den_out"), m.sem("wo_in"), m.sem("rw_in")
        inverted = m.sem("inverted")
        w_high, w_low = m.sem("wo_high"), m.sem("wo_low")
        consts = m.sem("consts1")
        a_in = [m.sem(f"a_in{s}") for s in range(SUB)]
        normed = m.sem("normed")
        a_high, a_low = m.sem("a_high"), m.sem("a_low")
        y_done = m.sem("y_done")
        step = m.sem("ln_step")
        std_done = m.sem("std_done")
        kept = m.sem("kept")
        tr_done = m.sem("tr_done")
        T_high, T_low = m.sem("T_high"), m.sem("T_low")
        rt_done = m.sem("rt_done")
        lT_taken = m.sem("lT_taken")
        back_done = m.sem("back_done")
        l_taken = m.sem("l_taken")
        block = ctx.enter_context(nc.Block("mix"))
        compact = lambda d: d.rearrange("n (a k) -> (n a) k", k=NH * S // P)

        @block.sync
        def _(sp):
            sp.dma_start(den_sb[:], compact(den)).then_inc(den_in, 16)
            sp.dma_start(w_raw[:], w_out.rearrange("(c p) n -> p c n", p=P)).then_inc(w_in, 16)
            sp.dma_start(r_raw[:], router_wT.rearrange("(c p) e -> p c e", p=P)).then_inc(r_in, 16)
            sp.wait_ge(inverted, 1)
            sp.dma_start(compact(rden), den_sb[:]).then_inc(den_out, 16)
            sp.wait_ge(den_out, 16)
            for g in range(NG):
                b, s = g // SUB, g % SUB
                cols = slice(s * G, (s + 1) * G)
                if b > 0:
                    sp.wait_ge(a_low, g - SUB + 1)
                    sp.wait_ge(step, 4 * STEPS + STEPS * TG * (g - SUB + 1))
                sp.dma_start(a_n[s][:], attn_T[b * D:(b + 1) * D, cols].rearrange("(c p) t -> p c t", p=P)).then_inc(a_in[s], 16)
                for h in range(H):
                    r0 = h * HD % P
                    sp.dma_start(a_rd[s][r0:r0 + HD, h * HD // P, :],
                                 rden[b * H + h:b * H + h + 1, cols].to_broadcast([HD, G])).then_inc(a_in[s], 16)
                sp.dma_start(x_nat[s][:], x[g * G:(g + 1) * G, :].rearrange("(t p) d -> p t d", p=P)).then_inc(a_in[s], 16)

        IN = 16 * (2 + H)

        @block.gpsimd
        def _(pool):
            pool.memset(f32(r_hi[:]), 0.0).then_inc(consts, 1)
            pool.memset(f32(r_lo[:]), 0.0).then_inc(consts, 1)
            pool.memset(eps[:], EPS).then_inc(consts, 1)

        @block.scalar
        def _(act):
            act.sem_inc(lT_taken, 1)
            act.sem_inc(l_taken, 1)
            act.sem_inc(kept, 4)
            act.wait_ge(w_in, 16)
            act.activation(w_hi[:], w_raw[:], ACT.Copy).then_inc(w_high, 1)
            act.wait_ge(r_in, 16)
            act.wait_ge(consts, 3)
            act.activation(r_hi[:, :, 0:E], r_raw[:], ACT.Copy).then_inc(w_high, 1)

            def high(g, s):
                act.wait_ge(normed, g + 1)
                act.wait_ge(y_done, TG * g + 4)
                act.activation(a_hi[s][:], a_n[s][:], ACT.Copy).then_inc(a_high, 1)

            def sigma(n, t):
                act.wait_ge(step, STEPS * (n + 4) + 3)
                act.activation(std[:, t % 4], mv[:, t % 4, 1:2], ACT.Sqrt, bias=eps[:]).then_inc(std_done, 1)

            def turned(b, t):
                act.wait_ge(tr_done, 4 + TB * b + t + 1)
                if t % TG == 0:
                    act.wait_ge(rt_done, SUB * b + t // TG + 1)
                act.activation(xT_hi[:, :, (t % TG) * P:(t % TG + 1) * P],
                               ps_t[:, t % 2].rearrange("p (c x) -> p c x", c=DC), ACT.Copy).then_inc(T_high, 1)

            def keep(n, t):
                act.wait_ge(step, STEPS * (n + 4) + 5)
                act.activation(x1_all[:, bass.ds(n, 1), :], x1[:, t % 4:t % 4 + 1], ACT.Copy).then_inc(kept, 1)

            def take_lT(g):
                act.wait_ge(rt_done, 1 + g + 1)
                act.wait_ge(back_done, g + 1)
                act.activation(lgT[:], ps_lT[0:E, :], ACT.Copy).then_inc(lT_taken, 1)

            def take_l(g):
                act.wait_ge(back_done, 1 + g + 1)
                act.activation(logits[:, bass.ds(g * TG, TG), :], ps_l[:, :, 0:E], ACT.Copy).then_inc(l_taken, 1)

            with act.Fori(0, B) as b:
                high(SUB * b, 0)
                for t in range(TB + LAG):
                    if t == 2:
                        high(SUB * b + 1, 1)
                    if t < TB:
                        sigma(TB * b + t, t)
                    if t >= LAG:
                        turned(b, t - LAG)
                    if 1 <= t <= TB:
                        keep(TB * b + t - 1, t - 1)
                    if t == TG + LAG - 1:
                        take_lT(SUB * b)
                    if t == TG + LAG:
                        take_l(SUB * b)
                take_lT(SUB * b + 1)
                take_l(SUB * b + 1)

        @block.vector
        def _(dve):
            dve.sem_inc(step, 4 * STEPS)
            dve.sem_inc(T_low, 2)
            dve.wait_ge(den_in, 16)
            dve.reciprocal(den_sb[:], den_sb[:]).then_inc(inverted, 1)
            dve.wait_ge(w_high, 1)
            dve.tensor_tensor(w_lo[:], w_raw[:], f32(w_hi[:]), ALU.subtract).then_inc(w_low, 1)
            dve.wait_ge(w_high, 2)
            dve.wait_ge(consts, 3)
            dve.tensor_tensor(r_lo[:, :, 0:E], r_raw[:], f32(r_hi[:, :, 0:E]), ALU.subtract).then_inc(w_low, 1)

            def divide(b, g, s):
                dve.wait_ge(a_in[s], IN * b + IN)
                dve.tensor_tensor(a_n[s][:], a_n[s][:], a_rd[s][:], ALU.mult).then_inc(normed, 1)

            def low(g, s):
                dve.wait_ge(a_high, g + 1)
                dve.tensor_tensor(a_lo[s][:], a_n[s][:], f32(a_hi[s][:]), ALU.subtract).then_inc(a_low, 1)

            def turned(n, t):
                dve.wait_ge(T_high, n + 1)
                at = slice((t % TG) * P, (t % TG + 1) * P)
                dve.tensor_tensor(xT_lo[:, :, at], ps_t[:, t % 2].rearrange("p (c x) -> p c x", c=DC),
                                  f32(xT_hi[:, :, at]), ALU.subtract).then_inc(T_low, 1)

            def norm(b, t):
                n, s, r = TB * b + t, t // TG, x1[:, t % 4, :]
                done = lambda k: STEPS * (n + 4) + k
                dve.wait_ge(y_done, 8 + n + 1)
                dve.wait_ge(tr_done, n + 1)
                dve.wait_ge(kept, n + 1)
                dve.tensor_tensor(r, ps_y[:, t % 4, :], x_nat[s][:, t % TG, :], ALU.add).then_inc(step, 1)
                dve.wait_ge(step, done(1))
                dve.bn_stats(stats[:, t % 4], r).then_inc(step, 1)
                count = value(dve, done(2))
                dve.wait_ge(inverted, 1)
                dve.wait_ge(step, count)
                dve.bn_aggr(mv[:, t % 4], stats[:, t % 4]).then_inc(step, 1)
                if t >= LAG:
                    turned(n - LAG, t - LAG)
                dve.wait_ge(std_done, n + 1)
                dve.reciprocal(rstd[:, t % 4], std[:, t % 4]).then_inc(step, 1)
                dve.wait_ge(step, done(4))
                dve.tensor_scalar(r, r, mv[:, t % 4, 0:1], rstd[:, t % 4], ALU.subtract, ALU.mult).then_inc(step, 1)

            with dve.Fori(0, B) as b:
                divide(b, SUB * b, 0)
                low(SUB * b, 0)
                for t in range(TB):
                    if t == 2:
                        divide(b, SUB * b + 1, 1)
                    norm(b, t)
                    if t == 2:
                        low(SUB * b + 1, 1)
                for t in range(TB - LAG, TB):
                    turned(TB * b + t, t)

        @block.tensor
        def _(pe):
            pe.sem_inc(y_done, 8)
            pe.sem_inc(tr_done, 4)
            pe.sem_inc(rt_done, 1)
            pe.sem_inc(back_done, 1)
            pe.wait_ge(w_low, 2)

            def out_project(b, t):
                s, tok = t // TG, slice((t % TG) * P, (t % TG + 1) * P)
                if t % TG == 0:
                    pe.wait_ge(a_low, SUB * b + s + 1)
                pe.wait_ge(step, STEPS * (TB * b + t) + 1)
                pairs = []
                for c in range(DC):
                    pairs += split3(a_hi[s][:, c, tok], a_lo[s][:, c, tok], w_hi[:, c, :], w_lo[:, c, :])
                product(pe, ps_y[:, t % 4, :], pairs).then_inc(y_done, 1)

            def turn(b, t):
                pe.wait_ge(step, STEPS * (TB * b + t + 4) + 5)
                pe.wait_ge(T_low, TB * b + t + 1)
                for c in range(DC):
                    tr = pe.transpose(ps_t[:, t % 2, c * P:(c + 1) * P], x1[:, t % 4, c * P:(c + 1) * P], ident[:])
                tr.then_inc(tr_done, 1)

            def route(b, s):
                pe.wait_ge(T_low, 2 + TB * b + TG * (s + 1))
                pe.wait_ge(lT_taken, SUB * b + s + 1)
                pairs = []
                for c in range(DC):
                    pairs += split3(r_hi[:, c, :], r_lo[:, c, :], xT_hi[:, c, :], xT_lo[:, c, :])
                product(pe, ps_lT[:], pairs).then_inc(rt_done, 1)

            def back(b, s):
                taken, free = value(pe, 1 + SUB * b + s + 1), value(pe, SUB * b + s + 1)
                pe.wait_ge(w_low, 2)
                pe.wait_ge(lT_taken, taken)
                pe.wait_ge(l_taken, free)
                for t in range(TG):
                    tr = pe.transpose(ps_l[:, t, 0:E], lgT[:, t * P:(t + 1) * P], ident[0:E, 0:E])
                tr.then_inc(back_done, 1)

            with pe.Fori(0, B) as b:
                for t in range(TB + LAG):
                    if t < TB:
                        out_project(b, t)
                    if t >= LAG:
                        turn(b, t - LAG)
                    if t == TG + LAG - 1:
                        route(b, 0)
                    if t == TG + LAG:
                        back(b, 0)
                route(b, 1)
                back(b, 1)


def route(nc, x1_all, logits, bias, xs_shared, slots, shares, tile_expert, ends):
    with ExitStack() as ctx:
        m = Mem(nc, ctx)
        bias_sb = m.sb("bias_sb", [P, E])
        u = [m.sb(f"route_u{k}", [P, NT, E]) for k in range(4)]
        score = m.sb("score", [P, NT, E])
        top = m.sb("top", [P, NT, 8])
        idx = m.sb("idx", [P, NT, 8], U32)
        idx_f = m.sb("idx_f", [P, NT, TOPK])
        iota_i = m.sb("iota_i", [P, E], I32)
        iota_f = m.sb("iota_f", [P, E])
        tile_i = m.sb("tile_i", [1, TILES_MAX], I32)
        tile_f = m.sb("tile_f", [1, TILES_MAX])
        hot = m.sb("hot", [P, NT, TOPK, E])
        picked = m.sb("picked", [P, NT, TOPK, E])
        chosen = m.sb("chosen", [P, NT, E], BF16)
        before = m.sb("before", [P, P], BF16)
        ones = m.sb("ones_r", [P, P], BF16)
        value_k = m.sb("value_k", [P, NT, TOPK])
        total = m.sb("total", [P, NT, 1])
        carry = m.sb("carry", [P, NT, E])
        number = m.sb("number", [P, E])
        number_i = m.sb("number_i", [P, E], I32)
        scan = [m.sb(f"scan{k}", [P, E]) for k in range(2)]
        starts = m.sb("starts", [P, E + 1])
        under = m.sb("under", [1, TILES_MAX, E])
        tile_q = m.sb("tile_q", [1, TILES_MAX])
        pairs_i = m.sb("pairs_i", [1, 2], I32)
        ps_rank = m.ps("ps_rank", [P, NT, E])
        ps_total = m.ps("ps_total", [P, NT, E])
        bias_in, shared_out = m.sem("bias_in"), m.sem("shared_out")
        consts = m.sem("consts2")
        did = m.sem("did")
        acted = m.sem("acted")
        counted = m.sem("counted")
        magnitude, one_plus, softplus = m.sem("magnitude"), m.sem("one_plus"), m.sem("softplus")
        chosen_done = m.sem("chosen_done")
        block = ctx.enter_context(nc.Block("route"))
        flat = "p t e -> p (t e)"

        @block.sync
        def _(sp):
            sp.dma_start(bias_sb[:], bias.to_broadcast([P, E])).then_inc(bias_in, 16)
            sp.dma_start(xs_shared.rearrange("(t p) d -> p t d", p=P), x1_all[:]).then_inc(shared_out, 16)
            sp.wait_ge(shared_out, 16)

        @block.gpsimd
        def _(pool):
            pool.iota(iota_i[:], [[1, E]], base=0, channel_multiplier=0).then_inc(consts, 1)
            pool.iota(tile_i[:], [[1, TILES_MAX]], base=0, channel_multiplier=0).then_inc(consts, 1)
            pool.memset(ones[:], 1.0).then_inc(consts, 1)
            pool.wait_ge(consts, 3)
            pool.affine_select(out=before[:], in_=ones[:], compare_op=ALU.is_gt, fill=0.0, base=0,
                               pattern=[[1, P]], channel_multiplier=-1).then_inc(consts, 1)

        @block.scalar
        def _(act):
            act.wait_ge(magnitude, 1)
            act.activation(u[1][:], u[0][:], ACT.Exp).then_inc(acted, 1)
            act.wait_ge(one_plus, 1)
            act.activation(u[3][:], u[2][:], ACT.Ln).then_inc(acted, 1)
            act.wait_ge(softplus, 1)
            act.activation(score[:], u[0][:], ACT.Sqrt).then_inc(acted, 1)

        @block.tensor
        def _(pe):
            pe.wait_ge(consts, 4)
            pe.wait_ge(chosen_done, 1)
            pe.matmul(ps_rank[:].rearrange(flat), before[:], chosen[:].rearrange(flat), start=True, stop=True).then_inc(counted, 1)
            pe.matmul(ps_total[:].rearrange(flat), ones[:], chosen[:].rearrange(flat), start=True, stop=True).then_inc(counted, 1)

        @block.vector
        def _(dve):
            steps = itertools.count(1).__next__

            dve.scalar_tensor_tensor(u[0][:], logits[:], -1.0, logits[:], ALU.mult, ALU.min).then_inc(did, 1)
            dve.wait_ge(did, steps())
            dve.sem_inc(magnitude, 1)
            dve.wait_ge(acted, 1)
            dve.tensor_scalar(u[2][:], u[1][:], 1.0, None, ALU.add).then_inc(did, 1)
            dve.wait_ge(did, steps())
            dve.sem_inc(one_plus, 1)
            less, small, series = picked[:, :, 0, :], picked[:, :, 1, :], picked[:, :, 2, :]
            dve.tensor_scalar(small, u[1][:], 1.0 / 64, None, ALU.is_lt).then_inc(did, 1)
            dve.wait_ge(did, steps())
            dve.tensor_scalar(series, u[1][:], -1.0 / 4, 1.0 / 3, ALU.mult, ALU.add).then_inc(did, 1)
            dve.wait_ge(did, steps())
            for c in (0.5, 1.0):
                dve.tensor_tensor(series, series, u[1][:], ALU.mult).then_inc(did, 1)
                dve.wait_ge(did, steps())
                dve.tensor_scalar(series, series, -1.0, c, ALU.mult, ALU.add).then_inc(did, 1)
                dve.wait_ge(did, steps())
            dve.tensor_tensor(series, series, u[1][:], ALU.mult).then_inc(did, 1)
            dve.wait_ge(did, steps())
            dve.tensor_scalar(less, u[2][:], 1.0, 1e-7, ALU.subtract, ALU.max).then_inc(did, 1)
            dve.wait_ge(did, steps())
            dve.reciprocal(u[0][:], less).then_inc(did, 1)
            dve.wait_ge(did, steps())
            dve.tensor_tensor(u[0][:], u[0][:], u[1][:], ALU.mult).then_inc(did, 1)
            dve.wait_ge(did, steps())
            dve.wait_ge(acted, 2)
            dve.tensor_tensor(u[0][:], u[0][:], u[3][:], ALU.mult).then_inc(did, 1)
            dve.wait_ge(did, steps())
            dve.tensor_tensor(series, series, u[0][:], ALU.subtract).then_inc(did, 1)
            dve.wait_ge(did, steps())
            dve.tensor_tensor(series, series, small, ALU.mult).then_inc(did, 1)
            dve.wait_ge(did, steps())
            dve.tensor_tensor(u[0][:], u[0][:], series, ALU.add).then_inc(did, 1)
            dve.wait_ge(did, steps())
            dve.scalar_tensor_tensor(u[0][:], logits[:], 0.0, u[0][:], ALU.max, ALU.add).then_inc(did, 1)
            dve.wait_ge(did, steps())
            dve.sem_inc(softplus, 1)

            dve.wait_ge(bias_in, 16)
            dve.wait_ge(acted, 3)
            dve.tensor_tensor(u[1][:], score[:], bias_sb[:].rearrange("p (o e) -> p o e", o=1).to_broadcast([P, NT, E]),
                              ALU.add).then_inc(did, 1)
            dve.wait_ge(did, steps())
            for t in range(NT):
                dve.max(top[:, t], u[1][:, t]).then_inc(did, 1)
                dve.wait_ge(did, steps())
                dve.max_index(idx[:, t], top[:, t], u[1][:, t]).then_inc(did, 1)
                dve.wait_ge(did, steps())
            dve.tensor_copy(idx_f[:], idx[:, :, 0:TOPK]).then_inc(did, 1)
            dve.wait_ge(did, steps())
            dve.wait_ge(consts, 4)
            dve.tensor_copy(iota_f[:], iota_i[:]).then_inc(did, 1)
            dve.wait_ge(did, steps())
            for k in range(TOPK):
                dve.tensor_tensor(hot[:, :, k, :], iota_f[:].rearrange("p (o e) -> p o e", o=1).to_broadcast([P, NT, E]),
                                  idx_f[:, :, k:k + 1].to_broadcast([P, NT, E]), ALU.is_equal).then_inc(did, 1)
                dve.wait_ge(did, steps())
            dve.tensor_tensor(u[2][:], hot[:, :, 0, :], hot[:, :, 1, :], ALU.add).then_inc(did, 1)
            dve.wait_ge(did, steps())
            dve.tensor_tensor(u[3][:], hot[:, :, 2, :], hot[:, :, 3, :], ALU.add).then_inc(did, 1)
            dve.wait_ge(did, steps())
            dve.tensor_tensor(chosen[:], u[2][:], u[3][:], ALU.add).then_inc(did, 1)
            dve.wait_ge(did, steps())
            dve.sem_inc(chosen_done, 1)

            dve.memset(carry[:, 0], 0.0).then_inc(did, 1)
            dve.wait_ge(did, steps())
            dve.wait_ge(counted, 2)
            for t in range(NT):
                out = carry[:, t + 1] if t + 1 < NT else number[:]
                dve.tensor_tensor(out, carry[:, t], ps_total[:, t], ALU.add).then_inc(did, 1)
                dve.wait_ge(did, steps())
            dve.tensor_scalar(number[:], number[:], float(P - 1), None, ALU.add).then_inc(did, 1)
            dve.wait_ge(did, steps())
            dve.tensor_copy(number_i[:], number[:]).then_inc(did, 1)
            dve.wait_ge(did, steps())
            dve.tensor_scalar(number_i[:], number_i[:], P.bit_length() - 1, None, ALU.arith_shift_right).then_inc(did, 1)
            dve.wait_ge(did, steps())
            dve.tensor_scalar(number_i[:], number_i[:], 1, None, ALU.max).then_inc(did, 1)
            dve.wait_ge(did, steps())
            dve.tensor_copy(scan[0][:], number_i[:]).then_inc(did, 1)
            dve.wait_ge(did, steps())
            d, src = 1, 0
            while d < E:
                dve.tensor_copy(scan[1 - src][:, 0:d], scan[src][:, 0:d]).then_inc(did, 1)
                dve.wait_ge(did, steps())
                dve.tensor_tensor(scan[1 - src][:, d:], scan[src][:, d:], scan[src][:, 0:E - d], ALU.add).then_inc(did, 1)
                dve.wait_ge(did, steps())
                d, src = 2 * d, 1 - src
            dve.memset(starts[:, 0:1], float(NT)).then_inc(did, 1)
            dve.wait_ge(did, steps())
            dve.tensor_scalar(starts[:, 1:], scan[src][:], float(NT), None, ALU.add).then_inc(did, 1)
            dve.wait_ge(did, steps())

            dve.scalar_tensor_tensor(carry[:], starts[:, 0:E].rearrange("p (o e) -> p o e", o=1).to_broadcast([P, NT, E]),
                                     float(P), carry[:], ALU.mult, ALU.add).then_inc(did, 1)
            dve.wait_ge(did, steps())
            dve.tensor_tensor(carry[:], carry[:], ps_rank[:], ALU.add).then_inc(did, 1)
            dve.wait_ge(did, steps())
            for k in range(TOPK):
                dve.tensor_tensor(picked[:, :, k, :], hot[:, :, k, :], carry[:], ALU.mult).then_inc(did, 1)
                dve.wait_ge(did, steps())
            dve.tensor_reduce(value_k[:], picked[:], AX.X, ALU.add).then_inc(did, 1)
            dve.wait_ge(did, steps())
            dve.tensor_copy(slots[:], value_k[:]).then_inc(did, 1)
            dve.wait_ge(did, steps())

            for k in range(TOPK):
                dve.tensor_tensor(picked[:, :, k, :], hot[:, :, k, :], score[:], ALU.mult).then_inc(did, 1)
                dve.wait_ge(did, steps())
            dve.tensor_reduce(value_k[:], picked[:], AX.X, ALU.add).then_inc(did, 1)
            dve.wait_ge(did, steps())
            dve.tensor_reduce(total[:, :, 0], value_k[:], AX.X, ALU.add).then_inc(did, 1)
            dve.wait_ge(did, steps())
            dve.tensor_scalar(total[:], total[:], 1e-20, None, ALU.add).then_inc(did, 1)
            dve.wait_ge(did, steps())
            dve.reciprocal(total[:], total[:]).then_inc(did, 1)
            dve.wait_ge(did, steps())
            dve.tensor_tensor(shares[:], value_k[:], total[:].to_broadcast([P, NT, TOPK]), ALU.mult).then_inc(did, 1)
            dve.wait_ge(did, steps())

            dve.tensor_copy(tile_f[:], tile_i[:]).then_inc(did, 1)
            dve.wait_ge(did, steps())
            dve.tensor_tensor(under[:], starts[0:1, 0:E].rearrange("p (o e) -> p o e", o=1).to_broadcast([1, TILES_MAX, E]),
                              tile_f[:].rearrange("p (t o) -> p t o", o=1).to_broadcast([1, TILES_MAX, E]),
                              ALU.is_le).then_inc(did, 1)
            dve.wait_ge(did, steps())
            dve.tensor_reduce(tile_q[:], under[:], AX.X, ALU.add).then_inc(did, 1)
            dve.wait_ge(did, steps())
            dve.tensor_copy(tile_expert[:], tile_q[:]).then_inc(did, 1)
            dve.wait_ge(did, steps())
            dve.tensor_copy(ends[:, 0:E + 1], starts[0:1, :]).then_inc(did, 1)
            dve.wait_ge(did, steps())
            dve.tensor_scalar(pairs_i[:, 0:1], ends[:, E:E + 1], 1, None, ALU.subtract).then_inc(did, 1)
            dve.wait_ge(did, steps())
            dve.tensor_scalar(ends[:, E + 1:E + 2], pairs_i[:, 0:1], 1, None, ALU.arith_shift_right).then_inc(did, 1)
            dve.wait_ge(did, steps())
            dve.tensor_scalar(ends[:, E + 2:E + 3], ends[:, E + 1:E + 2], -1, TILES_MAX // 2, ALU.mult, ALU.add).then_inc(did, 1)
            dve.wait_ge(did, steps())


def experts(nc, weights, x1_all, slots, xs, ys, ident, tile_expert, ends):
    with ExitStack() as ctx:
        m = Mem(nc, ctx)
        WB = 3
        NQ = E + 1
        w = m.sb("expert_w", [P, WB * WCOLS])
        xt = [m.sb(f"xt{p}", [P, D]) for p in range(2)]
        xT = [m.sb(f"xT{p}", [P, DC, P]) for p in range(2)]
        gu = [m.sb(f"gu{p}", [P, 2 * I]) for p in range(2)]
        act_g = [m.sb(f"act_g{p}", [P, I]) for p in range(2)]
        h = [m.sb(f"h{p}", [P, I]) for p in range(2)]
        hT = [m.sb(f"hT{p}", [P, IC, P]) for p in range(2)]
        y = [m.sb(f"y{p}", [P, D]) for p in range(2)]
        zeros = m.sb("zeros_e", [P, 2, D])
        ps_x = [m.ps(f"ps_x{p}", [P, D]) for p in range(2)]
        ps_gu = [m.ps(f"ps_gu{p}", [P, 2 * I]) for p in range(2)]
        ps_h = [m.ps(f"ps_h{p}", [P, IC, P]) for p in range(2)]
        ps_y = [m.ps(f"ps_e{p}", [P, D]) for p in range(2)]

        w_in = [m.sem(f"expert_w_in{r}") for r in range(WB)]
        w_ready = m.sem("w_ready")
        sent = m.sem("sent")
        zeroed, rest_out = m.sem("zeroed_e"), m.sem("rest_out")
        x_in = [m.sem(f"xt_in{p}") for p in range(2)]
        y_out = [m.sem(f"y_out{p}") for p in range(2)]
        xT_done = m.sem("xT_done")
        xT_taken = m.sem("xT_taken")
        gu_done = m.sem("gu_done")
        clipped = m.sem("clipped")
        gated = m.sem("gated")
        h_done = m.sem("h_done")
        hT_done = m.sem("hT_done")
        hT_taken = m.sem("hT_taken")
        y_done = m.sem("ye_done")
        y_taken = m.sem("y_taken")
        block = ctx.enter_context(nc.Block("experts"))

        def last_pair(eng):
            return eng.value_load(ends[0:1, E + 1:E + 2], min_val=(NT + E) // 2 - 1, max_val=TILES_MAX // 2 - 1)

        @block.gpsimd
        def _(pool):
            def load(q, r):
                pool.dma_start(w[:, r * WCOLS:(r + 1) * WCOLS], weights[:, bass.ds(q * WCOLS, WCOLS)]).then_inc(w_in[r], 16)

            def announce(j, r):
                pool.wait_ge(w_in[r], 16 * j + 16)
                pool.sem_inc(w_ready, 1)

            pool.memset(zeros[:], 0.0).then_inc(zeroed, 1)
            for q in range(WB):
                load(q, q)
            announce(0, 0)
            for t in range(NT):
                for k in range(TOPK):
                    pool.indirect_dma_start(xs, bass.IndirectOffsetOnAxis(ap=slots[:, t, k:k + 1], axis=0),
                                            x1_all[:, t, :], None).then_inc(sent, 16)
            last = last_pair(pool)
            unused = pool.value_load(ends[0:1, E + 2:E + 3], min_val=1, max_val=TILES_MAX // 2 + 1)
            pool.wait_ge(zeroed, 1)
            with pool.Fori(last + 1, TILES_MAX // 2 + 1) as j:
                pool.dma_start(ys[bass.ds(j * 2 * P, 2 * P), :].rearrange("(t p) d -> p t d", p=P),
                               zeros[:]).then_inc(rest_out, 16)
            stored = value(pool, unused * 16)
            pool.wait_ge(zeroed, 1)
            pool.wait_ge(rest_out, stored)
            with pool.Fori(1, NQ // WB) as j:
                for r in range(WB):
                    q = WB * j + r
                    announce(*((j, 0) if r == 2 else (j - 1, r + 1)))
                    end = pool.value_load(ends[0:1, bass.ds(q - WB, 1)], min_val=NT, max_val=TILES_MAX)
                    pool.wait_ge(y_done, end + 2)
                    load(q, r)
            announce(NQ // WB - 1, 1)
            announce(NQ // WB - 1, 2)

        @block.sync
        def _(sp):
            for p in range(2):
                sp.sem_inc(y_out[p], 16)

            def load(n, p):
                sp.dma_start(xt[p][:], xs[bass.ds(n * P, P), :]).then_inc(x_in[p], 16)

            def store(n, p):
                sp.wait_ge(y_taken, 2 + n + 1)
                sp.dma_start(ys[bass.ds(n * P, P), :], y[p][:]).then_inc(y_out[p], 16)

            load(0, 0)
            load(1, 1)
            sp.wait_ge(xT_done, 2 + 1)
            load(2, 0)
            sp.wait_ge(xT_done, 2 + 2)
            load(3, 1)
            store(0, 0)
            last = last_pair(sp)
            def pair(j):
                for p in range(2):
                    sp.wait_ge(xT_done, 2 * j + (3 + p))
                    load(2 * j + (2 + p), p)
                    store(2 * j + (p - 1), 1 - p)

            with sp.Fori(1, NT // 2 - 1) as j:
                pair(j)
            sp.wait_ge(x_in[0], 16)
            sp.wait_ge(sent, 16 * NT * TOPK)
            with sp.Fori(NT // 2 - 1, last) as j:
                pair(j)
            store(2 * last - 1, 1)
            store(2 * last, 0)
            store(2 * last + 1, 1)
            stored = value(sp, 16 * last + 32)
            sp.wait_ge(x_in[0], 16)
            for p in range(2):
                sp.wait_ge(y_out[p], stored)

        @block.scalar
        def _(act):
            act.sem_inc(xT_taken, 2)
            act.sem_inc(y_taken, 2)

            def take_x(n, p):
                act.wait_ge(xT_done, 2 + n + 1)
                act.wait_ge(gu_done, n + 1)
                act.activation(xT[p][:], ps_x[p][:].rearrange("p (c x) -> p c x", c=DC), ACT.Copy).then_inc(xT_taken, 1)

            def gate(n, p):
                act.wait_ge(clipped, 2 + n + 1)
                act.wait_ge(h_done, n + 1)
                act.activation(act_g[p][:], gu[p][:, 0:I], ACT.Silu).then_inc(gated, 1)

            def take_y(n, p, j):
                act.wait_ge(y_done, 2 + n + 1)
                act.wait_ge(y_out[p], 16 * j + 16)
                act.activation(y[p][:], ps_y[p][:], ACT.Copy).then_inc(y_taken, 1)

            take_x(0, 0)
            take_x(1, 1)
            gate(0, 0)
            last = last_pair(act)
            with act.Fori(0, last) as j:
                for p in range(2):
                    n = 2 * j + p
                    gate(n + 1, 1 - p)
                    take_x(n + 2, p)
                    take_y(n, p, j)
            gate(2 * last + 1, 1)
            take_y(2 * last, 0, last)
            take_y(2 * last + 1, 1, last)

        @block.vector
        def _(dve):
            dve.sem_inc(clipped, 2)
            dve.sem_inc(h_done, 2)
            dve.sem_inc(hT_taken, 2)
            with dve.Fori(0, last_pair(dve) + 1) as j:
                for p in range(2):
                    n = 2 * j + p
                    dve.wait_ge(gu_done, 2 + n + 1)
                    dve.wait_ge(h_done, n + 1)
                    dve.tensor_scalar(gu[p][:], ps_gu[p][:], ALPHA, -ALPHA, ALU.min, ALU.max).then_inc(clipped, 1)
                    dve.wait_ge(gated, n + 1)
                    dve.wait_ge(hT_done, n + 1)
                    dve.tensor_tensor(h[p][:], act_g[p][:], gu[p][:, I:], ALU.mult).then_inc(h_done, 1)
                    dve.wait_ge(hT_done, 2 + n + 1)
                    dve.wait_ge(y_done, n + 1)
                    dve.tensor_copy(hT[p][:], ps_h[p][:]).then_inc(hT_taken, 1)

        @block.tensor
        def _(pe):
            for s in (xT_done, gu_done, hT_done, y_done):
                pe.sem_inc(s, 2)

            def turn_x(n, p, j):
                pe.wait_ge(x_in[p], 16 * j + 16)
                pe.wait_ge(xT_taken, n + 1)
                for c in range(DC):
                    tr = pe.transpose(ps_x[p][:, c * P:(c + 1) * P], xt[p][:, c * P:(c + 1) * P], ident[:])
                tr.then_inc(xT_done, 1)

            def gate_up(n, p, q):
                pe.wait_ge(w_ready, q + 1)
                pe.wait_ge(xT_taken, 2 + n + 1)
                pe.wait_ge(clipped, n + 1)
                base = (q % WB) * WCOLS
                product(pe, ps_gu[p][:], [(xT[p][:, c, :], w[:, bass.ds(base + c * 2 * I, 2 * I)])
                                          for c in range(DC)]).then_inc(gu_done, 1)

            def turn_h(n, p):
                pe.wait_ge(h_done, 2 + n + 1)
                pe.wait_ge(hT_taken, n + 1)
                for c in range(IC):
                    tr = pe.transpose(ps_h[p][:, c, :], h[p][:, c * P:(c + 1) * P], ident[:])
                tr.then_inc(hT_done, 1)

            def down(n, p, q):
                pe.wait_ge(hT_taken, 2 + n + 1)
                pe.wait_ge(y_taken, n + 1)
                base = (q % WB) * WCOLS + DOWN0
                product(pe, ps_y[p][:], [(hT[p][:, c, :], w[:, bass.ds(base + c * D, D)])
                                         for c in range(IC)]).then_inc(y_done, 1)

            def expert_of(n):
                return pe.value_load(tile_expert[0:1, bass.ds(n, 1)], min_val=0, max_val=E)

            turn_x(0, 0, 0)
            gate_up(0, 0, 0)
            turn_x(1, 1, 0)
            last = last_pair(pe)
            with pe.Fori(0, last) as j:
                n = 2 * j
                q0, q1, q2 = expert_of(n), expert_of(n + 1), expert_of(n + 2)
                for t, qa, qb in ((0, q0, q1), (1, q1, q2)):
                    turn_h(2 * j + t, t)
                    gate_up(2 * j + (t + 1), 1 - t, qb)
                    turn_x(2 * j + (t + 2), t, j + 1)
                    down(2 * j + t, t, qa)
            n = 2 * last
            q0, q1 = expert_of(n), expert_of(n + 1)
            turn_h(n, 0)
            gate_up(n + 1, 1, q1)
            down(n, 0, q0)
            turn_h(n + 1, 1)
            down(n + 1, 1, q1)


def combine(nc, x1_all, ys_shared, ys_rows, slots, shares, out):
    with ExitStack() as ctx:
        m = Mem(nc, ctx)
        BUF, STEPS = 2, TOPK + 5
        yr = [m.sb(f"yr{p}", [P, TOPK, D]) for p in range(BUF)]
        yh = [m.sb(f"yh{p}", [P, D]) for p in range(BUF)]
        z = [m.sb(f"z{p}", [P, D]) for p in range(BUF)]
        stats = m.sb("stats2", [P, BUF, 6])
        mv = m.sb("mv2", [P, BUF, 2])
        std = m.sb("std2", [P, BUF, 1])
        rstd = m.sb("rstd2", [P, BUF, 1])
        eps = m.sb("eps2", [P, 1])
        gathered = [m.sem(f"gathered{p}") for p in range(BUF)]
        shared_in = [m.sem(f"shared_in{p}") for p in range(BUF)]
        z_out = [m.sem(f"z_out{p}") for p in range(BUF)]
        const = m.sem("const2")
        step = m.sem("combine_step")
        std_done = m.sem("std2_done")
        block = ctx.enter_context(nc.Block("combine"))
        rows = lambda d, t: d[t * P:(t + 1) * P, :]

        @block.sync
        def _(sp):
            for t in range(BUF):
                sp.dma_start(yh[t][:], rows(ys_shared, t)).then_inc(shared_in[t], 16)
            for t in range(NT):
                p = t % BUF
                sp.wait_ge(step, STEPS * (t + 1))
                sp.dma_start(rows(out, t), z[p][:]).then_inc(z_out[p], 16)
                if t + BUF < NT:
                    sp.dma_start(yh[p][:], rows(ys_shared, t + BUF)).then_inc(shared_in[p], 16)
            for p in range(BUF):
                sp.wait_ge(z_out[p], 16 * (NT // BUF))

        @block.gpsimd
        def _(pool):
            for t in range(NT):
                p = t % BUF
                if t >= BUF:
                    pool.wait_ge(step, STEPS * (t - BUF) + 1 + TOPK)
                for k in range(TOPK):
                    pool.indirect_dma_start(yr[p][:, k, :], None, ys_rows,
                                            bass.IndirectOffsetOnAxis(ap=slots[:, t, k:k + 1], axis=0)).then_inc(gathered[p], 16)

        @block.scalar
        def _(act):
            act.wait_ge(const, 1)
            for t in range(NT):
                p = t % BUF
                act.wait_ge(step, STEPS * t + TOPK + 3)
                act.activation(std[:, p], mv[:, p, 1:2], ACT.Sqrt, bias=eps[:]).then_inc(std_done, 1)

        @block.vector
        def _(dve):
            dve.memset(eps[:], EPS).then_inc(const, 1)
            for t in range(NT):
                p, n = t % BUF, STEPS * t
                if t >= BUF:
                    dve.wait_ge(z_out[p], 16 * (t // BUF))
                    dve.wait_ge(step, STEPS * (t - 1))
                dve.wait_ge(shared_in[p], 16 * (t // BUF) + 16)
                dve.tensor_tensor(z[p][:], x1_all[:, t, :], yh[p][:], ALU.add).then_inc(step, 1)
                dve.wait_ge(gathered[p], 16 * TOPK * (t // BUF + 1))
                for k in range(TOPK):
                    dve.wait_ge(step, n + 1 + k)
                    dve.scalar_tensor_tensor(z[p][:], yr[p][:, k, :], shares[:, t, k:k + 1], z[p][:],
                                             ALU.mult, ALU.add).then_inc(step, 1)
                dve.wait_ge(step, n + TOPK + 1)
                dve.bn_stats(stats[:, p], z[p][:]).then_inc(step, 1)
                dve.wait_ge(step, n + TOPK + 2)
                dve.bn_aggr(mv[:, p], stats[:, p]).then_inc(step, 1)
                dve.wait_ge(std_done, t + 1)
                dve.reciprocal(rstd[:, p], std[:, p]).then_inc(step, 1)
                dve.wait_ge(step, n + TOPK + 4)
                dve.tensor_scalar(z[p][:], z[p][:], mv[:, p, 0:1], rstd[:, p], ALU.subtract, ALU.mult).then_inc(step, 1)


def build(nc, xT, x, w_qkv, w_out, router_wT, bias, weights, out):
    dram = lambda name, shape: nc.dram_tensor(name, shape, F32, kind="Internal").ap()
    q_hi, q_lo, k_hi, k_lo = (dram(n, (B * D, S)) for n in ("q_hi", "q_lo", "k_hi", "k_lo"))
    attn_T, den, rden = dram("attn_T", (B * D, S)), dram("den", (NH, S)), dram("rden", (NH, S))
    xs, ys = dram("xs", (TILES_MAX * P, D)), dram("ys", ((TILES_MAX + 2) * P, D))
    with ExitStack() as ctx:
        v_all = ctx.enter_context(nc.sbuf_tensor("v_all", [P, KB, NH, HD], F32))
        project(nc, xT, w_qkv, q_hi, q_lo, k_hi, k_lo, v_all)
        attend(nc, q_hi, q_lo, k_hi, k_lo, v_all, attn_T, den, xs[T:, :])
    with ExitStack() as ctx:
        m = Mem(nc, ctx)
        ident = m.sb("ident", [P, P])
        x1_all = m.sb("x1_all", [P, NT, D])
        logits = m.sb("logits", [P, NT, E])
        slots = m.sb("slots", [P, NT, TOPK], U32)
        shares = m.sb("shares", [P, NT, TOPK])
        tile_expert = m.sb("tile_expert", [1, TILES_MAX], I32)
        ends = m.sb("ends", [1, E + 3], I32)
        made = m.sem("ident_made")
        with nc.Block("identity") as block:
            @block.gpsimd
            def _(pool):
                pool.memset(ident[:], 0.0).then_inc(made, 1)
                pool.wait_ge(made, 1)
                pool.affine_select(out=ident[:], in_=ident[:], compare_op=ALU.not_equal, fill=1.0, base=0,
                                   pattern=[[-1, P]], channel_multiplier=1).then_inc(made, 1)
        mix(nc, attn_T, den, rden, w_out, x, router_wT, ident, x1_all, logits)
        route(nc, x1_all, logits, bias, xs[0:T, :], slots, shares, tile_expert, ends)
        experts(nc, weights, x1_all, slots, xs, ys, ident, tile_expert, ends)
        combine(nc, x1_all, ys[0:T, :], ys, slots, shares, out)


def lay_out(gate, up, down):
    n = gate.shape[0]
    gu = np.concatenate([gate.transpose(0, 2, 1), up.transpose(0, 2, 1)], axis=2)
    gu = gu.reshape(n, DC, P, 2 * I).transpose(2, 0, 1, 3).reshape(P, n, DOWN0)
    dn = down.transpose(0, 2, 1).reshape(n, IC, P, D).transpose(2, 0, 1, 3).reshape(P, n, IC * D)
    return np.ascontiguousarray(np.concatenate([gu, dn], axis=2).reshape(P, n * WCOLS))


def kernel(L0_attn_x, L0_attn_w_qkv, L0_attn_w_out, L0_ffn_router_w, L0_ffn_expert_bias, L0_ffn_gate_w, L0_ffn_up_w,
           L0_ffn_down_w, L0_ffn_shared_gate_w, L0_ffn_shared_up_w, L0_ffn_shared_down_w):
    import concourse.bacc as _bacc
    from concourse.bass_utils import run_bass_kernel_spmd as _run

    x = np.asarray(L0_attn_x).reshape(T, D)
    stack = lambda shared, others: np.concatenate([np.asarray(shared)[None], np.asarray(others)])
    arrays = dict(
        xT=x.T, x=x, w_qkv=np.asarray(L0_attn_w_qkv), w_out=np.asarray(L0_attn_w_out),
        router_wT=np.asarray(L0_ffn_router_w).T, bias=np.asarray(L0_ffn_expert_bias).reshape(1, E),
        weights=lay_out(stack(L0_ffn_shared_gate_w, L0_ffn_gate_w), stack(L0_ffn_shared_up_w, L0_ffn_up_w),
                        stack(L0_ffn_shared_down_w, L0_ffn_down_w)))
    arrays = {f"in_{name}_dram": np.ascontiguousarray(a) for name, a in arrays.items()}
    nc = _bacc.Bacc("TRN2", target_bir_lowering=False, num_devices=1)
    args = [nc.dram_tensor(name, a.shape, F32, kind="ExternalInput").ap() for name, a in arrays.items()]
    out = nc.dram_tensor("out_0_dram", (T, D), F32, kind="ExternalOutput").ap()
    build(nc, *args, out)
    result = _run(nc, [arrays], core_ids=[0])
    return result.results[0]["out_0_dram"].reshape(B, S, D)
```

```python
import itertools
from contextlib import ExitStack

import numpy as np

import concourse.bass as bass
from concourse import mybir

F32 = mybir.dt.float32
F32R = mybir.dt.float32r
BF16 = mybir.dt.bfloat16
I32 = mybir.dt.int32
U32 = mybir.dt.uint32
ALU = mybir.AluOpType
ACT = mybir.ActivationFunctionType
AX = mybir.AxisListType

P = 128
B, S, D = 2, 1024, 512
H, HD = 16, 32
E, I, TOPK = 32, 256, 4
T = B * S
NT = T // P
DC = D // P
IC = I // P
NH = B * H
G = 512
NG = T // G
KB = S // P
WCOLS = DC * 2 * I + IC * D
DOWN0 = DC * 2 * I
TILES_MAX = NT + T * TOPK // P + E
EBASE = 64
ALPHA = 7.0
EPS = 1e-5
NEG = -1e30
INV_SQRT_HD = float(1.0 / np.sqrt(np.float32(HD)))

CHUNKS = [
    dict(group=1, st=[(0, 512, 512, 0), (1, 512, 512, 512)], cols=1024,
         pv=[(0, 0, 512, 0), (1, 512, 512, 0)], diag=None),
    dict(group=1, st=[(2, 512, 512, 0), (3, 512, 512, 512)], cols=1024,
         pv=[(2, 0, 512, 0), (3, 512, 512, 0)], diag=None),
    dict(group=1, st=[(4, 512, 512, 0), (5, 640, 384, 512)], cols=896,
         pv=[(4, 0, 512, 0), (5, 512, 384, 128)], diag=512),
    dict(group=1, st=[(6, 768, 256, 0), (7, 768, 256, 256)], cols=512,
         pv=[(6, 0, 256, 256), (7, 384, 128, 384)], diag=384),
    dict(group=0, st=[(0, 0, 512, 0), (1, 128, 384, 512)], cols=896,
         pv=[(0, 0, 512, 0), (1, 512, 384, 128)], diag=512),
    dict(group=0, st=[(2, 256, 256, 0), (3, 256, 256, 256)], cols=512,
         pv=[(2, 0, 256, 256), (3, 384, 128, 384)], diag=384),
]
NC_ = len(CHUNKS)
PIECES = [(t, 0, (t + 1) * P, True) for t in range(4)]
for _t in range(4, 8):
    PIECES += [(_t, 0, 512, False), (_t, 512, (_t - 3) * P, True)]
NP_ = len(PIECES)
SEQ = NP_ + 1


class Mem:

    def __init__(self, nc, ctx):
        self.nc, self.ctx = nc, ctx

    def sb(self, name, shape, dt=F32):
        return self.ctx.enter_context(self.nc.sbuf_tensor(name, shape, dt))

    def ps(self, name, shape, dt=F32):
        return self.ctx.enter_context(self.nc.psum_tensor(name, shape, dt))

    def sem(self, name):
        return self.ctx.enter_context(self.nc.semaphore(name))


def value(eng, n):
    return n if isinstance(n, int) else eng.to_reg(n)


def f32(ap):
    return ap.bitcast(F32)


def product(pe, out, pairs, first=True, last=True):
    for n, (l, r) in enumerate(pairs):
        mm = pe.matmul(out, l, r, start=(first and n == 0), stop=(last and n == len(pairs) - 1))
    return mm


def split3(lh, ll, rh, rl):
    return [(lh, rh), (lh, rl), (ll, rh)]


def project(nc, xT, w_qkv, q_hi, q_lo, k_hi, k_lo, v_all):
    with ExitStack() as ctx:
        m = Mem(nc, ctx)
        w_raw = m.sb("w_raw", [P, DC, 3 * D])
        w_hi = m.sb("w_hi", [P, DC, 3 * D], F32R)
        w_lo = m.sb("w_lo", [P, DC, 3 * D], F32R)
        x_raw = m.sb("x_raw", [P, NG, DC, G])
        x_hi = m.sb("x_hi", [P, 2, DC, G], F32R)
        x_lo = m.sb("x_lo", [P, 2, DC, G], F32R)
        out_hi = m.sb("out_hi", [P, 4, G], F32R)
        out_lo = m.sb("out_lo", [P, 4, G], F32R)
        acc = m.ps("acc_qkv", [P, 4, G])
        w_in = [m.sem(f"w_in{n}") for n in range(3)]
        x_in = [m.sem(f"x_in{s}") for s in range(2)]
        w_high, w_low = m.sem("w_high"), m.sem("w_low")
        kv_high, kv_low = m.sem("kv_high"), m.sem("kv_low")
        x_high, x_low = m.sem("x_high"), m.sem("x_low")
        made = m.sem("made")
        high = m.sem("high")
        low = m.sem("low")
        stored = [m.sem(f"stored{n}") for n in range(4)]
        block = ctx.enter_context(nc.Block("project"))
        NO = 12

        xT_v = xT.rearrange("(c p) t -> p c t", p=P)
        w_v = w_qkv.rearrange("(c p) n -> p c n", p=P)

        @block.sync
        def _(sp):
            for n in range(4):
                sp.sem_inc(stored[n], 32)
            for n in range(3):
                sp.dma_start(w_raw[:, :, n * D:(n + 1) * D], w_v[:, :, n * D:(n + 1) * D]).then_inc(w_in[n], 16)
                if n != 1:
                    s = n // 2
                    sp.dma_start(x_raw[:, s], xT_v[:, :, s * G:(s + 1) * G]).then_inc(x_in[s], 16)
            for s in range(2):
                sp.wait_ge(x_in[s], 16)
                sp.dma_start(x_raw[:, 2 + s], xT_v[:, :, (2 + s) * G:(3 + s) * G]).then_inc(x_in[s], 16)
            with sp.Fori(0, B) as b:
                for s in range(2):
                    for o in range(8):
                        hi_d, lo_d = (q_hi, q_lo) if o < 4 else (k_hi, k_lo)
                        n = 8 * (2 * b + s) + o + 1
                        rows = bass.ds(b * D + (o % 4) * P, P)
                        sp.wait_ge(high, n)
                        sp.dma_start(hi_d[rows, s * G:(s + 1) * G], f32(out_hi[:, o % 4])).then_inc(stored[o % 4], 16)
                        sp.wait_ge(low, 4 + NO * (2 * b + s) + o + 1)
                        sp.dma_start(lo_d[rows, s * G:(s + 1) * G], f32(out_lo[:, o % 4])).then_inc(stored[o % 4], 16)
            for n in range(4):
                sp.wait_ge(stored[n], 32 * (2 * NG + 1))

        @block.scalar
        def _(act):
            act.wait_ge(w_in[0], 16)
            act.activation(w_hi[:, :, 0:D], w_raw[:, :, 0:D], ACT.Copy).then_inc(w_high, 1)
            with act.Fori(0, B) as b:
                for s in range(2):
                    g = 2 * b + s
                    act.wait_ge(x_in[s], 16 * b + 16)
                    act.wait_ge(made, NO * (g + 1))
                    for c in range(DC):
                        act.activation(x_hi[:, s:s + 1, c], x_raw[:, bass.ds(g, 1), c], ACT.Copy).then_inc(x_high, 1)
                    for o in range(8):
                        act.wait_ge(made, 2 * NO + NO * g + o + 1)
                        act.wait_ge(stored[o % 4], 32 * (2 * g + o // 4 + 1))
                        act.activation(out_hi[:, o % 4], acc[:, o % 4], ACT.Copy,
                                       scale=INV_SQRT_HD if o < 4 else 1.0).then_inc(high, 1)

        @block.vector
        def _(dve):
            dve.sem_inc(low, 4)

            dve.wait_ge(w_high, 1)
            dve.tensor_tensor(w_lo[:, :, 0:D], w_raw[:, :, 0:D], f32(w_hi[:, :, 0:D]), ALU.subtract).then_inc(w_low, 1)
            with dve.Fori(0, B) as b:
                for s in range(2):
                    g = 2 * b + s
                    for c in range(DC):
                        dve.wait_ge(x_high, DC * g + c + 1)
                        dve.tensor_tensor(x_lo[:, s:s + 1, c], x_raw[:, bass.ds(g, 1), c], f32(x_hi[:, s:s + 1, c]),
                                          ALU.subtract).then_inc(x_low, 1)
                    for o in range(8):
                        dve.wait_ge(high, 8 * g + o + 1)
                        dve.wait_ge(stored[o % 4], 32 * (2 * g + o // 4 + 1))
                        dve.scalar_tensor_tensor(out_lo[:, o % 4], acc[:, o % 4], INV_SQRT_HD if o < 4 else 1.0,
                                                 f32(out_hi[:, o % 4]), ALU.mult, ALU.subtract).then_inc(low, 1)
                    for t in range(4):
                        dve.wait_ge(made, 2 * NO + NO * g + 8 + t + 1)
                        dve.tensor_copy(v_all[:, 4 * s + t, bass.ds(b * H, H), :],
                                        acc[:, t].rearrange("p (h d) -> p h d", d=HD)).then_inc(low, 1)

        @block.gpsimd
        def _(pool):
            for n in range(1, 3):
                part = slice(n * D, (n + 1) * D)
                pool.wait_ge(w_in[n], 16)
                pool.tensor_copy(w_hi[:, :, part], w_raw[:, :, part]).then_inc(kv_high, 1)
                pool.wait_ge(kv_high, n)
                pool.tensor_tensor(w_lo[:, :, part], w_raw[:, :, part], f32(w_hi[:, :, part]), ALU.subtract).then_inc(kv_low, 1)

        @block.tensor
        def _(pe):
            pe.sem_inc(made, 2 * NO)
            pe.wait_ge(w_low, 1)
            with pe.Fori(0, B) as b:
                for s in range(2):
                    g = 2 * b + s
                    for o in range(12):
                        pe.wait_ge(low, NO * g + o + 1)
                        if o in (4, 8):
                            pe.wait_ge(kv_low, o // 4)
                        for c in range(DC):
                            if o == 0:
                                pe.wait_ge(x_low, DC * g + c + 1)
                            if o < 8:
                                col = slice((o // 4) * D + (o % 4) * P, (o // 4) * D + (o % 4 + 1) * P)
                                pairs = split3(w_hi[:, c, col], w_lo[:, c, col], x_hi[:, s, c], x_lo[:, s, c])
                            else:
                                tok = slice((o - 8) * P, (o - 7) * P)
                                pairs = split3(x_hi[:, s, c, tok], x_lo[:, s, c, tok],
                                               w_hi[:, c, 2 * D:], w_lo[:, c, 2 * D:])
                            mm = product(pe, acc[:, o % 4], pairs, c == 0, c == DC - 1)
                        mm.then_inc(made, 1)


def attend(nc, q_hi, q_lo, k_hi, k_lo, v_all, attn_T, den, xs_zero):
    with ExitStack() as ctx:
        m = Mem(nc, ctx)
        SETUP = 13
        RING = 4
        qs = [m.sb(f"qs{r}", [3 * HD + 1, S], F32R) for r in range(RING)]
        ks = [m.sb(f"ks{r}", [3 * HD + 1, S], F32R) for r in range(RING)]
        vs = [m.sb(f"vs{p}", [P, KB, 2 * HD]) for p in range(2)]
        mask = m.sb("mask", [P, 512])
        mx = [m.sb(f"mx{p}", [P, KB]) for p in range(2)]
        mx2 = [m.sb(f"mx2{p}", [P, 8]) for p in range(2)]
        neg_row = [m.sb(f"neg_row{r}", [KB, P], F32R) for r in range(RING)]
        ident = m.sb("ident_a", [P, P])
        probs = [m.sb(f"probs{r}", [P, 1024]) for r in range(3)]
        o_sb = [[m.sb(f"o{p}{g}", [HD + 1, 512]) for g in range(2)] for p in range(2)]
        zeros = m.sb("zeros", [P, D])
        ps_st = [m.ps(f"ps_st{r}", [P, 1024]) for r in range(2)]
        ps_s = [m.ps(f"ps_s{r}", [P, 512]) for r in range(2)]
        ps_o = [m.ps(f"ps_o{g}", [P, 512]) for g in range(2)]

        loaded = [m.sem(f"loaded{r}") for r in range(RING)]
        row_in = [m.sem(f"row_in{r}") for r in range(RING)]
        st_done = m.sem("st_done")
        s_done = m.sem("s_done")
        pv_done = m.sem("pv_done")
        exp_done = m.sem("exp_done")
        row_done = m.sem("row_done")
        masked = m.sem("masked")
        v_done = m.sem("v_done")
        s_taken = m.sem("s_taken")
        max_done = m.sem("max_done")
        o_done = m.sem("o_done")
        o_out = [[m.sem(f"o_out{p}{g}") for g in range(2)] for p in range(2)]
        setup = m.sem("setup")
        zeroed = [m.sem(f"zeroed{p}") for p in range(2)]
        block = ctx.enter_context(nc.Block("attend"))

        def load(sp, i, r):
            rows = bass.ds(i * HD, HD)
            for n, (qd, kd) in enumerate(((q_hi, k_hi), (q_hi, k_lo), (q_lo, k_hi))):
                sp.dma_start(f32(qs[r][n * HD:(n + 1) * HD, :]), qd[rows, :]).then_inc(loaded[r], 16)
                sp.dma_start(f32(ks[r][n * HD:(n + 1) * HD, :]), kd[rows, :]).then_inc(loaded[r], 16)

        @block.sync
        def _(sp):
            for r in range(RING):
                sp.sem_inc(row_in[r], 16)
            for p in range(2):
                for g in range(2):
                    sp.sem_inc(o_out[p][g], 32)
                sp.sem_inc(zeroed[p], 16)

            def send_row(j, r):
                sp.wait_ge(row_done, RING * j + (r + 1))
                sp.dma_start(f32(qs[r % RING][3 * HD:3 * HD + 1, :].rearrange("o (t x) -> o t x", x=P)),
                             f32(neg_row[r % RING][:, :])).then_inc(row_in[r % RING], 16)

            def store(i, p, g):
                cols = slice(g * 512, (g + 1) * 512)
                count = value(sp, 2 + 2 * i + (1 if g == 1 else 2))
                sp.wait_ge(loaded[p], 96)
                sp.wait_ge(o_done, count)
                sp.dma_start(attn_T[bass.ds(i * HD, HD), cols], o_sb[p][g][0:HD, :]).then_inc(o_out[p][g], 16)
                sp.dma_start(den[bass.ds(i, 1), cols], o_sb[p][g][HD:HD + 1, :]).then_inc(o_out[p][g], 16)

            def zero(i, p):
                rows = xs_zero.shape[0] // NH
                q = max(d for d in range(1, P + 1) if rows % d == 0)
                sp.dma_start(xs_zero[bass.ds(i * rows, rows), :].rearrange("(n q) d -> q n d", q=q),
                             zeros[0:q].rearrange("q (o d) -> q o d", o=1).to_broadcast([q, rows // q, D])).then_inc(zeroed[p], 16)

            def head(j, r):
                i, p = RING * j + r, r % 2
                static = isinstance(j, int)
                if not static:
                    sp.wait_ge(st_done, NC_ * (i + 1))
                    load(sp, i + RING, r)
                for g in (1, 0):
                    store(i, p, g)
                if not static or r + 2 < RING:
                    send_row(j, r + 2)
                sp.wait_ge(zeroed[p], 16 * (2 * j + r // 2) + 16)
                zero(i, p)

            for r in range(RING):
                load(sp, r, r)
            for r in range(2):
                send_row(0, r)
            with sp.Fori(0, NH // RING - 1) as j:
                for r in range(RING):
                    head(j, r)
            for r in range(RING):
                head(NH // RING - 1, r)
            for p in range(2):
                for g in range(2):
                    sp.wait_ge(o_out[p][g], 32 * (NH // 2 + 1))
                sp.wait_ge(zeroed[p], 16 * (NH // 2 + 1))

        @block.gpsimd
        def _(pool):
            pool.memset(zeros[:], 0.0).then_inc(setup, 1)
            pool.memset(ident[:], 0.0).then_inc(setup, 1)
            pool.memset(mask[:], 0.0).then_inc(setup, 1)
            for p in range(2):
                pool.memset(vs[p][:, :, HD:], 1.0).then_inc(setup, 1)
            pool.wait_ge(setup, 5)
            pool.affine_select(out=ident[:], in_=ident[:], compare_op=ALU.not_equal, fill=1.0, base=0,
                               pattern=[[-1, P]], channel_multiplier=1).then_inc(setup, 1)
            pool.affine_select(out=mask[:, 384:], in_=mask[:, 384:], compare_op=ALU.is_ge, fill=NEG, base=0,
                               pattern=[[-1, P]], channel_multiplier=1).then_inc(setup, 1)

            def values(i, p):
                if not isinstance(i, int) or i >= 2:
                    pool.wait_ge(pv_done, 12 + NC_ * (i - 1))
                pool.tensor_copy(vs[p][:, :, 0:HD].rearrange("p k (o d) -> p k o d", o=1),
                                 v_all[:, :, bass.ds(i, 1), :]).then_inc(v_done, 1)

            def masks(i):
                for k in range(2, NC_):
                    gap = CHUNKS[k]["diag"]
                    count = value(pool, 2 + NC_ * i + k + 1)
                    pool.wait_ge(setup, SETUP)
                    pool.wait_ge(exp_done, count)
                    at = probs[k % 3][:, 0:2 * gap].rearrange("p (a x) -> p a x", a=2)[:, :, 0:P]
                    pool.affine_select(out=at, in_=at, compare_op=ALU.is_ge, fill=0.0, base=0,
                                       pattern=[[0, 2], [1, P]], channel_multiplier=-1).then_inc(masked, 1)

            values(0, 0)
            with pool.Fori(0, NH // 2 - 1) as j:
                for p in range(2):
                    values(2 * j + (p + 1), 1 - p)
                    masks(2 * j + p)
            values(NH - 1, 1)
            masks(NH - 2)
            masks(NH - 1)

        @block.scalar
        def _(act):
            act.sem_inc(exp_done, 2)

            def row(j, r):
                slot = (SEQ * (r % 2) + NP_) % 2
                act.wait_ge(s_done, SEQ * (RING * j + r) + SEQ)
                act.wait_ge(row_in[r % RING], 16 * (j + r // RING) + 16)
                act.activation(neg_row[r % RING][:, :], ps_s[slot][0:KB, 0:P], ACT.Copy, scale=-1.0).then_inc(row_done, 1)

            def head(j, r):
                i = RING * j + r
                if not (isinstance(i, int) and i == NH - 1):
                    row(j, r + 1)
                for k in range(NC_):
                    n = CHUNKS[k]["cols"]
                    act.wait_ge(st_done, NC_ * i + k + 1)
                    act.wait_ge(pv_done, NC_ * i + k + 10)
                    act.activation(probs[k % 3][:, 0:n], ps_st[k % 2][:, 0:n], ACT.Exp).then_inc(exp_done, 1)

            row(0, 0)
            with act.Fori(0, NH // RING - 1) as j:
                for r in range(RING):
                    head(j, r)
            for r in range(RING):
                head(NH // RING - 1, r)

        @block.vector
        def _(dve):
            dve.sem_inc(o_done, 2)
            dve.wait_ge(setup, 7)
            for r in range(RING):
                dve.memset(f32(ks[r][3 * HD:3 * HD + 1, :]), 1.0).then_inc(setup, 1)
            for p in range(2):
                dve.memset(mx2[p][:], NEG).then_inc(setup, 1)

            def maxima(i, p, q0, q1):
                for q in range(q0, q1):
                    t, k0, w, diag = PIECES[q]
                    bank = ps_s[(SEQ * p + q) % 2][:, 0:w]
                    out = mx[p][:, t:t + 1] if t < 4 or not diag else mx2[p][:, t:t + 1]
                    count = value(dve, SEQ * i + q + 1)
                    if diag:
                        dve.wait_ge(setup, SETUP)
                    dve.wait_ge(s_done, count)
                    if diag:
                        dve.tensor_tensor_reduce(bank, bank, mask[:, 512 - w:], 1.0, -3e38, ALU.add, ALU.max,
                                                 out).then_inc(s_taken, 1)
                    else:
                        dve.tensor_reduce(out, bank, AX.X, ALU.max).then_inc(s_taken, 1)
                if q1 == NP_:
                    dve.wait_ge(s_taken, NP_ * (i + 1))
                    dve.tensor_tensor(mx[p][:, 4:8], mx[p][:, 4:8], mx2[p][:, 4:8], ALU.max).then_inc(max_done, 1)

            def output(j, r, g):
                p = r % 2
                dve.wait_ge(o_out[p][g], 32 * (2 * j + r // 2) + 32)
                dve.wait_ge(pv_done, 12 + NC_ * (RING * j + r) + (4 if g == 1 else 6))
                dve.tensor_copy(o_sb[p][g][:, :], ps_o[g][0:HD + 1, :]).then_inc(o_done, 1)

            def head(j, r, ahead):
                if ahead:
                    maxima(RING * j + (r + 2), r % 2, 0, 10)
                output(j, r, 1)
                if ahead:
                    maxima(RING * j + (r + 2), r % 2, 10, NP_)
                output(j, r, 0)

            for i in range(2):
                maxima(i, i, 0, NP_)
            with dve.Fori(0, NH // RING - 1) as j:
                for r in range(RING):
                    head(j, r, True)
            for r in range(RING):
                head(NH // RING - 1, r, r + 2 < RING)

        @block.tensor
        def _(pe):
            def piece(j, r, q):
                i, p = RING * j + r, r % 2
                first = isinstance(i, int) and i == 0
                t, k0, w, _ = PIECES[q]
                w = max(w, 2 * P)
                if q == 0:
                    pe.wait_ge(loaded[r % RING], 96 * (j + r // RING) + 96)
                    if not first:
                        pe.wait_ge(s_taken, NP_ * i)
                elif q == 1:
                    if not first:
                        pe.wait_ge(row_done, i)
                else:
                    pe.wait_ge(s_taken, NP_ * i + q - 1)
                pe.matmul(ps_s[(SEQ * p + q) % 2][:, 0:w], qs[r % RING][0:3 * HD, t * P:(t + 1) * P],
                          ks[r % RING][0:3 * HD, k0:k0 + w], start=True, stop=True).then_inc(s_done, 1)

            def turn(j, r):
                p = r % 2
                pe.wait_ge(max_done, RING * j + (r + 1))
                pe.transpose(ps_s[(SEQ * p + NP_) % 2][0:KB, 0:P], mx[p][:, :], ident[:]).then_inc(s_done, 1)

            def scores_T(j, r, k):
                if k == 0:
                    pe.wait_ge(row_in[r], 16 * j + 32)
                pe.wait_ge(exp_done, NC_ * (RING * j + r) + k + 1)
                for kb, q0, w, col in CHUNKS[k]["st"]:
                    mm = pe.matmul(ps_st[k % 2][:, col:col + w], ks[r][:, kb * P:(kb + 1) * P],
                                   qs[r][:, q0:q0 + w], start=True, stop=True)
                mm.then_inc(st_done, 1)

            def values(j, r, k):
                i, p = RING * j + r, r % 2
                g = CHUNKS[k]["group"]
                if k == 0:
                    pe.wait_ge(v_done, i + 1)
                    pe.wait_ge(o_done, 2 * i + 1)
                if k == 4:
                    pe.wait_ge(o_done, 2 * i + 2)
                if k < 2:
                    pe.wait_ge(exp_done, 2 + NC_ * i + k + 1)
                else:
                    pe.wait_ge(masked, 4 * i + k - 1)
                pv = CHUNKS[k]["pv"]
                for n, (kb, col, w, q0) in enumerate(pv):
                    mm = pe.matmul(ps_o[g][0:2 * HD, q0:q0 + w], vs[p][:, kb, :], probs[k % 3][:, col:col + w],
                                   start=(kb == 0), stop=(k in (3, 5) and n == 1), skip_group_check=True)
                mm.then_inc(pv_done, 1)

            def head(j, r, turning, ahead):
                for k in range(NC_):
                    if k == 0 and turning:
                        turn(j, r + 1)
                    if ahead:
                        piece(j, r + 2, 2 * k)
                    scores_T(j, r, k)
                    if ahead:
                        piece(j, r + 2, 2 * k + 1)
                    if k > 0:
                        values(j, r, k - 1)
                values(j, r, NC_ - 1)

            pe.sem_inc(pv_done, 12)
            pe.wait_ge(setup, SETUP)
            for q in range(NP_):
                piece(0, 0, q)
            turn(0, 0)
            for q in range(NP_):
                piece(0, 1, q)
            with pe.Fori(0, NH // RING - 1) as j:
                for r in range(RING):
                    head(j, r, True, True)
            for r in range(RING):
                head(NH // RING - 1, r, r + 1 < RING, r + 2 < RING)


def mix(nc, attn_T, den, rden, w_out, x, router_wT, ident, x1_all, logits):
    with ExitStack() as ctx:
        m = Mem(nc, ctx)
        SUB = S // G
        TB = S // P
        TG = G // P
        LAG = 2
        STEPS = 5
        den_sb = m.sb("den_sb", [P, NH * S // P])
        w_raw = m.sb("wo_raw", [P, DC, D])
        w_hi = m.sb("wo_hi", [P, DC, D], F32R)
        w_lo = m.sb("wo_lo", [P, DC, D], F32R)
        r_raw = m.sb("rw_raw", [P, DC, E])
        r_hi = m.sb("rw_hi", [P, DC, P], F32R)
        r_lo = m.sb("rw_lo", [P, DC, P], F32R)
        a_n = [m.sb(f"a_n{s}", [P, DC, G]) for s in range(SUB)]
        a_rd = [m.sb(f"a_rd{s}", [P, DC, G]) for s in range(SUB)]
        a_hi = [m.sb(f"a_hi{s}", [P, DC, G], F32R) for s in range(SUB)]
        a_lo = [m.sb(f"a_lo{s}", [P, DC, G], F32R) for s in range(SUB)]
        x_nat = [m.sb(f"x_nat{s}", [P, TG, D]) for s in range(SUB)]
        x1 = m.sb("x1_new", [P, 4, D])
        xT_hi = m.sb("x1T_hi", [P, DC, G], F32R)
        xT_lo = m.sb("x1T_lo", [P, DC, G], F32R)
        lgT = m.sb("lgT", [E, G])
        stats = m.sb("stats1", [P, 4, 6])
        mv = m.sb("mv1", [P, 4, 2])
        std = m.sb("std1", [P, 4, 1])
        rstd = m.sb("rstd1", [P, 4, 1])
        eps = m.sb("eps1", [P, 1])
        ps_y = m.ps("ps_y", [P, 4, D])
        ps_t = m.ps("ps_t", [P, 2, D])
        ps_lT = m.ps("ps_lT", [P, G])
        ps_l = m.ps("ps_l", [P, TG, P])

        den_in, den_out, w_in, r_in = m.sem("den_in"), m.sem("den_out"), m.sem("wo_in"), m.sem("rw_in")
        inverted = m.sem("inverted")
        w_high, w_low = m.sem("wo_high"), m.sem("wo_low")
        consts = m.sem("consts1")
        a_in = [m.sem(f"a_in{s}") for s in range(SUB)]
        x_in = [m.sem(f"x_nat_in{s}") for s in range(SUB)]
        normed = m.sem("normed")
        a_high, a_low = m.sem("a_high"), m.sem("a_low")
        y_done = m.sem("y_done")
        step = m.sem("ln_step")
        std_done = m.sem("std_done")
        kept = m.sem("kept")
        tr_done = m.sem("tr_done")
        T_high, T_low = m.sem("T_high"), m.sem("T_low")
        rt_done = m.sem("rt_done")
        lT_taken = m.sem("lT_taken")
        back_done = m.sem("back_done")
        l_taken = m.sem("l_taken")
        block = ctx.enter_context(nc.Block("mix"))
        compact = lambda d: d.rearrange("n (a k) -> (n a) k", k=NH * S // P)

        @block.sync
        def _(sp):
            sp.dma_start(den_sb[:], compact(den)).then_inc(den_in, 16)
            sp.dma_start(w_raw[:], w_out.rearrange("(c p) n -> p c n", p=P)).then_inc(w_in, 16)
            sp.dma_start(r_raw[:], router_wT.rearrange("(c p) e -> p c e", p=P)).then_inc(r_in, 16)
            sp.wait_ge(inverted, 1)
            sp.dma_start(compact(rden), den_sb[:]).then_inc(den_out, 16)
            for g in range(NG):
                b, s = g // SUB, g % SUB
                cols = slice(s * G, (s + 1) * G)
                if b > 0:
                    sp.wait_ge(a_low, DC * (g - SUB + 1))
                sp.dma_start(a_n[s][:], attn_T[b * D:(b + 1) * D, cols].rearrange("(c p) t -> p c t", p=P)).then_inc(a_in[s], 16)
                if g == 0:
                    sp.wait_ge(den_out, 16)
                if b > 0:
                    sp.wait_ge(step, 4 * STEPS + STEPS * TG * (g - SUB + 1))
                for c in range(DC):
                    heads = rden[b * H + c * (H // DC):b * H + (c + 1) * (H // DC), cols]
                    sp.dma_start(a_rd[s][:, c, :], heads.rearrange("h (o t) -> h o t", o=1).to_broadcast([H // DC, HD, G])).then_inc(a_in[s], 16)
                sp.dma_start(x_nat[s][:], x[g * G:(g + 1) * G, :].rearrange("(t p) d -> p t d", p=P)).then_inc(x_in[s], 16)

        IN = 16 * (1 + DC)

        @block.gpsimd
        def _(pool):
            pool.memset(f32(r_hi[:]), 0.0).then_inc(consts, 1)
            pool.memset(f32(r_lo[:]), 0.0).then_inc(consts, 1)
            pool.memset(eps[:], EPS).then_inc(consts, 1)

        @block.scalar
        def _(act):
            act.sem_inc(lT_taken, 1)
            act.sem_inc(l_taken, 1)
            act.sem_inc(kept, 4)
            act.wait_ge(w_in, 16)
            act.activation(w_hi[:], w_raw[:], ACT.Copy).then_inc(w_high, 1)
            act.wait_ge(r_in, 16)
            act.wait_ge(consts, 3)
            act.activation(r_hi[:, :, 0:E], r_raw[:], ACT.Copy).then_inc(w_high, 1)

            def high(g, s):
                for c in range(DC):
                    act.wait_ge(normed, DC * g + c + 1)
                    if c == 0:
                        act.wait_ge(y_done, TG * g + 4)
                    act.activation(a_hi[s][:, c], a_n[s][:, c], ACT.Copy).then_inc(a_high, 1)

            def sigma(n, t):
                act.wait_ge(step, STEPS * (n + 4) + 3)
                act.activation(std[:, t % 4], mv[:, t % 4, 1:2], ACT.Sqrt, bias=eps[:]).then_inc(std_done, 1)

            def turned(b, t):
                act.wait_ge(tr_done, 4 + TB * b + t + 1)
                if t % TG == 0:
                    act.wait_ge(rt_done, SUB * b + t // TG + 1)
                act.activation(xT_hi[:, :, (t % TG) * P:(t % TG + 1) * P],
                               ps_t[:, t % 2].rearrange("p (c x) -> p c x", c=DC), ACT.Copy).then_inc(T_high, 1)

            def keep(n, t):
                act.wait_ge(step, STEPS * (n + 4) + 5)
                act.activation(x1_all[:, bass.ds(n, 1), :], x1[:, t % 4:t % 4 + 1], ACT.Copy).then_inc(kept, 1)

            def take_lT(g):
                act.wait_ge(rt_done, 1 + g + 1)
                act.wait_ge(back_done, g + 1)
                act.activation(lgT[:], ps_lT[0:E, :], ACT.Copy).then_inc(lT_taken, 1)

            def take_l(g):
                act.wait_ge(back_done, 1 + g + 1)
                act.activation(logits[:, bass.ds(g * TG, TG), :], ps_l[:, :, 0:E], ACT.Copy).then_inc(l_taken, 1)

            with act.Fori(0, B) as b:
                high(SUB * b, 0)
                high(SUB * b + 1, 1)
                for t in range(TB + LAG):
                    if t >= LAG:
                        turned(b, t - LAG)
                    if t < TB:
                        sigma(TB * b + t, t)
                    if 1 <= t <= TB:
                        keep(TB * b + t - 1, t - 1)
                    if t == TG + LAG:
                        take_lT(SUB * b)
                    if t == TG + LAG + 1:
                        take_l(SUB * b)
                take_lT(SUB * b + 1)
                take_l(SUB * b + 1)

        @block.vector
        def _(dve):
            dve.sem_inc(step, 4 * STEPS)
            dve.sem_inc(T_low, 2)
            dve.wait_ge(den_in, 16)
            dve.reciprocal(den_sb[:], den_sb[:]).then_inc(inverted, 1)
            dve.wait_ge(w_high, 1)
            dve.tensor_tensor(w_lo[:], w_raw[:], f32(w_hi[:]), ALU.subtract).then_inc(w_low, 1)
            dve.wait_ge(w_high, 2)
            dve.wait_ge(consts, 3)
            dve.tensor_tensor(r_lo[:, :, 0:E], r_raw[:], f32(r_hi[:, :, 0:E]), ALU.subtract).then_inc(w_low, 1)

            def divide(b, g, s):
                dve.wait_ge(a_in[s], IN * b + IN)
                for c in range(DC):
                    dve.tensor_tensor(a_n[s][:, c], a_n[s][:, c], a_rd[s][:, c], ALU.mult).then_inc(normed, 1)

            def low(g, s):
                for c in range(DC):
                    dve.wait_ge(a_high, DC * g + c + 1)
                    dve.tensor_tensor(a_lo[s][:, c], a_n[s][:, c], f32(a_hi[s][:, c]), ALU.subtract).then_inc(a_low, 1)

            def turned(n, t):
                dve.wait_ge(T_high, n + 1)
                at = slice((t % TG) * P, (t % TG + 1) * P)
                dve.tensor_tensor(xT_lo[:, :, at], ps_t[:, t % 2].rearrange("p (c x) -> p c x", c=DC),
                                  f32(xT_hi[:, :, at]), ALU.subtract).then_inc(T_low, 1)

            def norm(b, t):
                n, s, r = TB * b + t, t // TG, x1[:, t % 4, :]
                done = lambda k: STEPS * (n + 4) + k
                dve.wait_ge(y_done, 8 + n + 1)
                dve.wait_ge(tr_done, n + 1)
                dve.wait_ge(kept, n + 1)
                if t % TG == 0:
                    dve.wait_ge(x_in[s], 16 * b + 16)
                dve.tensor_tensor(r, ps_y[:, t % 4, :], x_nat[s][:, t % TG, :], ALU.add).then_inc(step, 1)
                dve.wait_ge(step, done(1))
                dve.bn_stats(stats[:, t % 4], r).then_inc(step, 1)
                count = value(dve, done(2))
                dve.wait_ge(inverted, 1)
                dve.wait_ge(step, count)
                dve.bn_aggr(mv[:, t % 4], stats[:, t % 4]).then_inc(step, 1)
                if t >= LAG:
                    turned(n - LAG, t - LAG)
                dve.wait_ge(std_done, n + 1)
                dve.reciprocal(rstd[:, t % 4], std[:, t % 4]).then_inc(step, 1)
                dve.wait_ge(step, done(4))
                dve.tensor_scalar(r, r, mv[:, t % 4, 0:1], rstd[:, t % 4], ALU.subtract, ALU.mult).then_inc(step, 1)

            with dve.Fori(0, B) as b:
                divide(b, SUB * b, 0)
                low(SUB * b, 0)
                divide(b, SUB * b + 1, 1)
                for t in range(TB):
                    norm(b, t)
                    if t == 0:
                        low(SUB * b + 1, 1)
                for t in range(TB - LAG, TB):
                    turned(TB * b + t, t)

        @block.tensor
        def _(pe):
            pe.sem_inc(y_done, 8)
            pe.sem_inc(tr_done, 4)
            pe.sem_inc(rt_done, 1)
            pe.sem_inc(back_done, 1)
            pe.wait_ge(w_low, 2)

            def out_project(b, t):
                s, tok = t // TG, slice((t % TG) * P, (t % TG + 1) * P)
                pe.wait_ge(step, STEPS * (TB * b + t) + 1)
                for c in range(DC):
                    if t % TG == 0:
                        pe.wait_ge(a_low, DC * (SUB * b + s) + c + 1)
                    mm = product(pe, ps_y[:, t % 4, :],
                                 split3(a_hi[s][:, c, tok], a_lo[s][:, c, tok], w_hi[:, c, :], w_lo[:, c, :]),
                                 c == 0, c == DC - 1)
                mm.then_inc(y_done, 1)

            def turn(b, t):
                pe.wait_ge(step, STEPS * (TB * b + t + 4) + 5)
                pe.wait_ge(T_low, TB * b + t + 1)
                for c in range(DC):
                    tr = pe.transpose(ps_t[:, t % 2, c * P:(c + 1) * P], x1[:, t % 4, c * P:(c + 1) * P], ident[:])
                tr.then_inc(tr_done, 1)

            def route(b, s):
                pe.wait_ge(T_low, 2 + TB * b + TG * (s + 1))
                pe.wait_ge(lT_taken, SUB * b + s + 1)
                pairs = []
                for c in range(DC):
                    pairs += split3(r_hi[:, c, :], r_lo[:, c, :], xT_hi[:, c, :], xT_lo[:, c, :])
                product(pe, ps_lT[:], pairs).then_inc(rt_done, 1)

            def back(b, s):
                taken, free = value(pe, 1 + SUB * b + s + 1), value(pe, SUB * b + s + 1)
                pe.wait_ge(w_low, 2)
                pe.wait_ge(lT_taken, taken)
                pe.wait_ge(l_taken, free)
                for t in range(TG):
                    tr = pe.transpose(ps_l[:, t, 0:E], lgT[:, t * P:(t + 1) * P], ident[0:E, 0:E])
                tr.then_inc(back_done, 1)

            with pe.Fori(0, B) as b:
                for t in range(TB + LAG):
                    if t < TB:
                        out_project(b, t)
                    if t == TG + LAG:
                        route(b, 0)
                    if t >= LAG:
                        turn(b, t - LAG)
                    if t == TG + LAG + 1:
                        back(b, 0)
                route(b, 1)
                back(b, 1)


def route(nc, ident, x1_all, logits, bias, xs_shared, slots, score, hot, tile_expert, ends, weights, bufs):
    with ExitStack() as ctx:
        m = Mem(nc, ctx)
        bias_sb = m.sb("bias_sb", [P, E])
        u = [m.sb(f"route_u{k}", [P, NT, E]) for k in range(4)]
        top = m.sb("top", [P, NT, 8])
        idx = m.sb("idx", [P, NT, 8], U32)
        idx_f = m.sb("idx_f", [P, NT, TOPK])
        iota_i = m.sb("iota_i", [P, E], I32)
        iota_f = m.sb("iota_f", [P, E])
        tile_i = m.sb("tile_i", [P, 1], I32)
        tile_f = m.sb("tile_f", [P, 1])
        picked = m.sb("picked", [P, NT, TOPK, E])
        chosen = m.sb("chosen", [P, NT, E], BF16)
        before = m.sb("before", [P, P], BF16)
        ones = m.sb("ones_r", [P, P], BF16)
        value_k = m.sb("value_k", [P, NT, TOPK])
        row_of = m.sb("row_of", [P, NT, E])
        number = m.sb("number", [P, E])
        number_i = m.sb("number_i", [P, E], I32)
        scan = [m.sb(f"scan{k}", [P, E]) for k in range(2)]
        starts = m.sb("starts", [P, E + 1])
        under = m.sb("under", [P, E])
        tile_q = m.sb("tile_q", [P, 1])
        row_q = m.sb("row_q", [1, TILES_MAX // 2 + 1, 2])
        two = m.sb("two", [1, TILES_MAX // 2 + 1])
        pairs_i = m.sb("pairs_i", [1, 2], I32)
        ps_rank = m.ps("ps_rank", [P, NT, E])
        ps_number = m.ps("ps_number", [P, 4 * P])
        ps_row = m.ps("ps_row", [P, 4 * P])
        bias_in, shared_out = m.sem("bias_in"), m.sem("shared_out")
        consts = m.sem("consts2")
        w_in = [m.sem(f"w_first{r}") for r in range(2)]
        x_in = [m.sem(f"x_first{r}") for r in range(2)]
        w_high, w_low = m.sem("w_first_high"), m.sem("w_first_low")
        w_at = [slice(q * WCOLS, (q + 1) * WCOLS) for q in range(2)]
        did = m.sem("did")
        acted = m.sem("acted")
        counted = m.sem("counted")
        magnitude, one_plus, softplus = m.sem("magnitude"), m.sem("one_plus"), m.sem("softplus")
        chosen_done, tiles_known = m.sem("chosen_done"), m.sem("tiles_known")
        block = ctx.enter_context(nc.Block("route"))
        flat = "p t e -> p (t e)"

        @block.sync
        def _(sp):
            sp.dma_start(bias_sb[:], bias.to_broadcast([P, E])).then_inc(bias_in, 16)
            sp.dma_start(xs_shared.rearrange("(t p) d -> p t d", p=P), x1_all[:]).then_inc(shared_out, 16)
            for q in range(2):
                sp.dma_start(bufs.w_raw[q][:], weights[:, w_at[q]]).then_inc(w_in[q], 16)
            sp.wait_ge(shared_out, 16)
            for t in range(2):
                sp.dma_start(bufs.xt[:, t * D:(t + 1) * D], xs_shared[t * P:(t + 1) * P, :]).then_inc(x_in[t], 16)
            for t in range(2):
                sp.wait_ge(x_in[t], 16)

        @block.gpsimd
        def _(pool):
            pool.iota(iota_i[:], [[1, E]], base=0, channel_multiplier=0).then_inc(consts, 1)
            pool.iota(tile_i[:], [[1, 1]], base=0, channel_multiplier=1).then_inc(consts, 1)
            pool.memset(ones[:], 1.0).then_inc(consts, 1)
            pool.wait_ge(consts, 3)
            pool.affine_select(out=before[:], in_=ones[:], compare_op=ALU.is_gt, fill=0.0, base=0,
                               pattern=[[1, P]], channel_multiplier=-1).then_inc(consts, 1)
            for q in range(2):
                pool.wait_ge(w_high, q + 1)
                pool.tensor_tensor(bufs.w_lo[:, w_at[q]], bufs.w_raw[q][:], f32(bufs.w_hi[:, w_at[q]]),
                                   ALU.subtract).then_inc(w_low, 1)
            pool.wait_ge(w_low, 2)

        @block.scalar
        def _(act):
            act.wait_ge(magnitude, 1)
            act.activation(u[1][:], u[0][:], ACT.Exp).then_inc(acted, 1)
            act.wait_ge(one_plus, 1)
            act.activation(u[3][:], u[2][:], ACT.Ln).then_inc(acted, 1)
            act.wait_ge(softplus, 1)
            act.activation(score[:], u[0][:], ACT.Sqrt).then_inc(acted, 1)
            for q in range(2):
                act.wait_ge(w_in[q], 16)
                act.activation(bufs.w_hi[:, w_at[q]], bufs.w_raw[q][:], ACT.Copy).then_inc(w_high, 1)

        @block.tensor
        def _(pe):
            pe.wait_ge(consts, 4)
            pe.wait_ge(chosen_done, 1)
            for t in range(NT):
                mm = pe.matmul(ps_number[:, 0:E], ones[:], chosen[:, t, :], start=(t == 0), stop=(t == NT - 1))
            mm.then_inc(counted, 1)
            pe.matmul(ps_rank[:].rearrange(flat), before[:], chosen[:].rearrange(flat), start=True, stop=True)
            for t in range(NT - 1):
                mm = pe.matmul(ps_rank[:, t + 1:, :], ones[:], chosen[:, t:t + 1, :].to_broadcast([P, NT - 1 - t, E]),
                               start=False, stop=True, skip_group_check=True)
            mm.then_inc(counted, 1)
            pe.wait_ge(tiles_known, 1)
            pe.matmul(ps_row[0:1, 0:P], tile_q[:], ident[:], start=True, stop=True).then_inc(counted, 1)

        @block.vector
        def _(dve):
            steps = itertools.count(1).__next__

            dve.scalar_tensor_tensor(u[0][:], logits[:], -1.0, logits[:], ALU.mult, ALU.min).then_inc(did, 1)
            dve.wait_ge(did, steps())
            dve.sem_inc(magnitude, 1)
            dve.wait_ge(acted, 1)
            dve.tensor_scalar(u[2][:], u[1][:], 1.0, None, ALU.add).then_inc(did, 1)
            dve.wait_ge(did, steps())
            dve.sem_inc(one_plus, 1)
            less, small, series = picked[:, :, 0, :], picked[:, :, 1, :], picked[:, :, 2, :]
            dve.tensor_scalar(small, u[1][:], 1.0 / 64, None, ALU.is_lt).then_inc(did, 1)
            dve.wait_ge(did, steps())
            dve.tensor_scalar(series, u[1][:], -1.0 / 4, 1.0 / 3, ALU.mult, ALU.add).then_inc(did, 1)
            dve.wait_ge(did, steps())
            for c in (0.5, 1.0):
                dve.tensor_tensor(series, series, u[1][:], ALU.mult).then_inc(did, 1)
                dve.wait_ge(did, steps())
                dve.tensor_scalar(series, series, -1.0, c, ALU.mult, ALU.add).then_inc(did, 1)
                dve.wait_ge(did, steps())
            dve.tensor_tensor(series, series, u[1][:], ALU.mult).then_inc(did, 1)
            dve.wait_ge(did, steps())
            dve.tensor_scalar(less, u[2][:], 1.0, 1e-7, ALU.subtract, ALU.max).then_inc(did, 1)
            dve.wait_ge(did, steps())
            dve.reciprocal(u[0][:], less).then_inc(did, 1)
            dve.wait_ge(did, steps())
            dve.tensor_tensor(u[0][:], u[0][:], u[1][:], ALU.mult).then_inc(did, 1)
            dve.wait_ge(did, steps())
            dve.wait_ge(acted, 2)
            dve.tensor_tensor(u[0][:], u[0][:], u[3][:], ALU.mult).then_inc(did, 1)
            dve.wait_ge(did, steps())
            dve.tensor_tensor(series, series, u[0][:], ALU.subtract).then_inc(did, 1)
            dve.wait_ge(did, steps())
            dve.tensor_tensor(series, series, small, ALU.mult).then_inc(did, 1)
            dve.wait_ge(did, steps())
            dve.tensor_tensor(u[0][:], u[0][:], series, ALU.add).then_inc(did, 1)
            dve.wait_ge(did, steps())
            dve.scalar_tensor_tensor(u[0][:], logits[:], 0.0, u[0][:], ALU.max, ALU.add).then_inc(did, 1)
            dve.wait_ge(did, steps())
            dve.sem_inc(softplus, 1)

            dve.wait_ge(bias_in, 16)
            dve.wait_ge(acted, 3)
            dve.tensor_tensor(u[1][:], score[:], bias_sb[:].rearrange("p (o e) -> p o e", o=1).to_broadcast([P, NT, E]),
                              ALU.add).then_inc(did, 1)
            dve.wait_ge(did, steps())
            for t in range(NT):
                dve.max(top[:, t], u[1][:, t]).then_inc(did, 1)
                n = steps()
            dve.wait_ge(did, n)
            for t in range(NT):
                dve.max_index(idx[:, t], top[:, t], u[1][:, t]).then_inc(did, 1)
                n = steps()
            dve.wait_ge(did, n)
            dve.tensor_copy(idx_f[:], idx[:, :, 0:TOPK]).then_inc(did, 1)
            dve.wait_ge(did, steps())
            dve.wait_ge(consts, 4)
            dve.tensor_copy(iota_f[:], iota_i[:]).then_inc(did, 1)
            dve.wait_ge(did, steps())
            dve.tensor_tensor(hot[:], iota_f[:].rearrange("p (o q e) -> p o q e", o=1, q=1).to_broadcast([P, NT, TOPK, E]),
                              idx_f[:].rearrange("p t (k o) -> p t k o", o=1).to_broadcast([P, NT, TOPK, E]), ALU.is_equal).then_inc(did, 1)
            dve.wait_ge(did, steps())
            dve.tensor_tensor(u[2][:], hot[:, :, 0, :], hot[:, :, 1, :], ALU.add).then_inc(did, 1)
            steps()
            dve.tensor_tensor(u[3][:], hot[:, :, 2, :], hot[:, :, 3, :], ALU.add).then_inc(did, 1)
            dve.wait_ge(did, steps())
            dve.tensor_tensor(chosen[:], u[2][:], u[3][:], ALU.add).then_inc(did, 1)
            dve.wait_ge(did, steps())
            dve.sem_inc(chosen_done, 1)

            dve.wait_ge(counted, 1)
            dve.tensor_scalar(number[:], ps_number[:, 0:E], float(P - 1), None, ALU.add).then_inc(did, 1)
            dve.wait_ge(did, steps())
            dve.tensor_copy(number_i[:], number[:]).then_inc(did, 1)
            dve.wait_ge(did, steps())
            dve.tensor_scalar(number_i[:], number_i[:], P.bit_length() - 1, None, ALU.arith_shift_right).then_inc(did, 1)
            dve.wait_ge(did, steps())
            dve.tensor_scalar(number_i[:], number_i[:], 1, None, ALU.max).then_inc(did, 1)
            dve.wait_ge(did, steps())
            dve.tensor_copy(scan[0][:], number_i[:]).then_inc(did, 1)
            dve.wait_ge(did, steps())
            d, src = 1, 0
            while d < E:
                dve.tensor_copy(scan[1 - src][:, 0:d], scan[src][:, 0:d]).then_inc(did, 1)
                dve.wait_ge(did, steps())
                dve.tensor_tensor(scan[1 - src][:, d:], scan[src][:, d:], scan[src][:, 0:E - d], ALU.add).then_inc(did, 1)
                dve.wait_ge(did, steps())
                d, src = 2 * d, 1 - src
            dve.memset(starts[:, 0:1], float(NT)).then_inc(did, 1)
            dve.wait_ge(did, steps())
            dve.tensor_scalar(starts[:, 1:], scan[src][:], float(NT), None, ALU.add).then_inc(did, 1)
            dve.wait_ge(did, steps())

            dve.wait_ge(counted, 2)
            dve.scalar_tensor_tensor(row_of[:], starts[:, 0:E].rearrange("p (o e) -> p o e", o=1).to_broadcast([P, NT, E]),
                                     float(P), ps_rank[:], ALU.mult, ALU.add).then_inc(did, 1)
            dve.wait_ge(did, steps())
            dve.tensor_tensor(picked[:], hot[:], row_of[:].rearrange("p t (o e) -> p t o e", o=1).to_broadcast([P, NT, TOPK, E]),
                              ALU.mult).then_inc(did, 1)
            dve.wait_ge(did, steps())
            dve.tensor_reduce(value_k[:], picked[:], AX.X, ALU.add).then_inc(did, 1)
            dve.wait_ge(did, steps())
            dve.tensor_copy(slots[:], value_k[:]).then_inc(did, 1)
            dve.wait_ge(did, steps())

            dve.tensor_copy(tile_f[:], tile_i[:]).then_inc(did, 1)
            dve.wait_ge(did, steps())
            dve.tensor_scalar(under[:], starts[:, 0:E], tile_f[:, 0:1], None, ALU.is_le).then_inc(did, 1)
            dve.wait_ge(did, steps())
            dve.tensor_reduce(tile_q[:], under[:], AX.X, ALU.add).then_inc(did, 1)
            dve.wait_ge(did, steps())
            dve.sem_inc(tiles_known, 1)
            dve.wait_ge(counted, 3)
            dve.tensor_copy(row_q[:].rearrange("p j t -> p (j t)"), ps_row[0:1, 0:TILES_MAX + 2]).then_inc(did, 1)
            dve.wait_ge(did, steps())
            dve.scalar_tensor_tensor(two[:], row_q[:, :, 1], float(EBASE), row_q[:, :, 0], ALU.mult, ALU.add).then_inc(did, 1)
            dve.wait_ge(did, steps())
            dve.scalar_tensor_tensor(tile_expert[:], two[:, 1:], float(EBASE ** 2), two[:, :-1], ALU.mult, ALU.add).then_inc(did, 1)
            dve.wait_ge(did, steps())
            dve.tensor_copy(ends[:, 0:E + 1], starts[0:1, :]).then_inc(did, 1)
            dve.wait_ge(did, steps())
            dve.tensor_scalar(pairs_i[:, 0:1], ends[:, E:E + 1], 1, None, ALU.subtract).then_inc(did, 1)
            dve.wait_ge(did, steps())
            dve.tensor_scalar(ends[:, E + 1:E + 2], pairs_i[:, 0:1], 1, None, ALU.arith_shift_right).then_inc(did, 1)
            dve.wait_ge(did, steps())
            dve.tensor_scalar(ends[:, E + 2:E + 3], ends[:, E + 1:E + 2], -1, TILES_MAX // 2, ALU.mult, ALU.add).then_inc(did, 1)
            dve.wait_ge(did, steps())


WB = 4


class ExpertBuffers:

    def __init__(self, m):
        self.w_raw = [m.sb(f"w_raw{r}", [P, WCOLS]) for r in range(2)]
        self.w_hi = m.sb("expert_w_hi", [P, WB * WCOLS], F32R)
        self.w_lo = m.sb("expert_w_lo", [P, WB * WCOLS], F32R)
        self.xt = m.sb("xt", [P, 2 * D])


def experts(nc, weights, bufs, x1_all, slots, xs, ys, ident, tile_expert, ends):
    with ExitStack() as ctx:
        m = Mem(nc, ctx)
        NQ = E + 1
        w_raw, w_hi, w_lo, xt = bufs.w_raw, bufs.w_hi, bufs.w_lo, bufs.xt
        xT_hi, xT_lo = m.sb("xT_hi", [P, 2 * D], F32R), m.sb("xT_lo", [P, 2 * D], F32R)
        gu = m.sb("gu", [P, 2 * 2 * I])
        act_g = m.sb("act_g", [P, 2 * I])
        h = m.sb("h", [P, 2 * I])
        hT_hi, hT_lo = m.sb("hT_hi", [P, 2 * I], F32R), m.sb("hT_lo", [P, 2 * I], F32R)
        y = m.sb("y", [P, 2 * D])
        zeros = m.sb("zeros_e", [P, 2, D])
        ps_x = m.ps("ps_x", [P, 2 * D])
        ps_gu = m.ps("ps_gu", [P, 2 * 2 * I])
        ps_h = m.ps("ps_h", [P, 2 * D])
        ps_y = m.ps("ps_e", [P, 2 * D])

        w_in = [m.sem(f"expert_w_in{r}") for r in range(2)]
        raw_ready = m.sem("raw_ready")
        w_high = m.sem("expert_w_high")
        w_low = m.sem("expert_w_low")
        sent = m.sem("sent")
        zeroed, rest_out = m.sem("zeroed_e"), m.sem("rest_out")
        x_in = [m.sem(f"xt_in{p}") for p in range(2)]
        y_out = [m.sem(f"y_out{p}") for p in range(2)]
        xT_done = m.sem("xT_done")
        x_high = m.sem("xT_high")
        x_low = m.sem("xT_low")
        gu_done = m.sem("gu_done")
        clipped = m.sem("clipped")
        gated = m.sem("gated")
        h_done = m.sem("h_done")
        hT_done = m.sem("hT_done")
        h_high = m.sem("hT_high")
        h_low = m.sem("hT_low")
        y_done = m.sem("ye_done")
        y_taken = m.sem("y_taken")
        y_free = m.sem("y_free")
        block = ctx.enter_context(nc.Block("experts"))

        def last_pair(eng):
            return eng.value_load(ends[0:1, E + 1:E + 2], min_val=(NT + E) // 2 - 1, max_val=TILES_MAX // 2 - 1)

        def half(n, size):
            return bass.ds((n % 2) * size, size)

        def source(q):
            return weights[:, bass.ds(q * WCOLS, WCOLS)]

        @block.gpsimd
        def _(pool):
            def load(q, r):
                pool.dma_start(w_raw[r][:], source(q)).then_inc(w_in[r], 16)

            def low(q, r):
                pool.wait_ge(w_high, q + 1)
                pool.tensor_tensor(w_lo[:, bass.ds((q % WB) * WCOLS, WCOLS)], w_raw[r][:],
                                   f32(w_hi[:, bass.ds((q % WB) * WCOLS, WCOLS)]), ALU.subtract).then_inc(w_low, 1)

            def expert(j, r, more):
                pool.wait_ge(w_in[r], 16 * j)
                pool.sem_inc(raw_ready, 1)
                low(2 * j + r, r)
                if more:
                    pool.wait_ge(w_low, 2 * j + (r + 1))
                    load(2 * j + (r + 2), r)

            pool.memset(zeros[:], 0.0).then_inc(zeroed, 1)
            pool.sem_inc(w_low, 2)
            for r in range(2):
                load(2 + r, r)
            for t in range(NT):
                for k in range(TOPK):
                    pool.indirect_dma_start(xs, bass.IndirectOffsetOnAxis(ap=slots[:, t, k:k + 1], axis=0),
                                            x1_all[:, t, :], None).then_inc(sent, 16)
            last = last_pair(pool)
            unused = pool.value_load(ends[0:1, E + 2:E + 3], min_val=1, max_val=TILES_MAX // 2 + 1)
            pool.wait_ge(zeroed, 1)
            with pool.Fori(last + 1, TILES_MAX // 2 + 1) as j:
                pool.dma_start(ys[bass.ds(j * 2 * P, 2 * P), :].rearrange("(t p) d -> p t d", p=P),
                               zeros[:]).then_inc(rest_out, 16)
            with pool.Fori(1, NQ // 2 - 1) as j:
                for r in range(2):
                    expert(j, r, True)
            expert(NQ // 2 - 1, 0, True)
            expert(NQ // 2 - 1, 1, False)
            expert(NQ // 2, 0, False)
            stored = value(pool, unused * 16)
            pool.wait_ge(zeroed, 1)
            pool.wait_ge(rest_out, stored)

        @block.sync
        def _(sp):
            for p in range(2):
                sp.sem_inc(y_out[p], 16)
                sp.sem_inc(x_in[p], 16)
            sp.sem_inc(y_free, 2)

            def load(n, p):
                sp.dma_start(xt[:, p * D:(p + 1) * D], xs[bass.ds(n * P, P), :]).then_inc(x_in[p], 16)

            def store(i, p):
                sp.wait_ge(y_out[p], 16 * i + 16)
                sp.sem_inc(y_free, 1)
                sp.wait_ge(y_taken, 2 * i + (p + 3))
                sp.dma_start(ys[bass.ds((2 * i + p) * P, P), :], y[:, p * D:(p + 1) * D]).then_inc(y_out[p], 16)

            def pair(j):
                for p in range(2):
                    sp.wait_ge(xT_done, 2 * j + (3 + p))
                    load(2 * j + (2 + p), p)
                    store(j - 2, p)

            for n in range(4):
                sp.wait_ge(xT_done, 2 + n + 1)
                load(n + 2, n % 2)
            with sp.Fori(2, NT // 2 - 1) as j:
                pair(j)
            sp.wait_ge(x_in[0], 16)
            sp.wait_ge(sent, 16 * NT * TOPK)
            last = last_pair(sp)
            with sp.Fori(NT // 2 - 1, last + 1) as j:
                pair(j)
            for i in (last - 1, last):
                for p in range(2):
                    store(i, p)
            stored, loaded = value(sp, 16 * last + 32), value(sp, 16 * last + 32)
            sp.wait_ge(x_in[0], 16)
            for p in range(2):
                sp.wait_ge(y_out[p], stored)
                sp.wait_ge(x_in[p], loaded)

        @block.scalar
        def _(act):
            act.sem_inc(y_taken, 2)

            def high(q, raw):
                act.activation(w_hi[:, bass.ds((q % WB) * WCOLS, WCOLS)], raw[:], ACT.Copy).then_inc(w_high, 1)

            def x_part(n):
                act.wait_ge(xT_done, n + 3)
                act.wait_ge(gu_done, n + 1)
                act.activation(xT_hi[:, half(n, D)], ps_x[:, half(n, D)], ACT.Copy).then_inc(x_high, 1)

            def gate(n):
                act.wait_ge(clipped, n + 3)
                act.wait_ge(h_done, n + 1)
                act.activation(act_g[:, half(n, I)], gu[:, bass.ds((n % 2) * 2 * I, I)], ACT.Silu).then_inc(gated, 1)

            def h_part(n):
                act.wait_ge(hT_done, n + 2)
                act.wait_ge(y_done, n)
                act.activation(hT_hi[:, half(n + 1, I)], ps_h[:, bass.ds(((n + 1) % 2) * D, I)], ACT.Copy).then_inc(h_high, 1)

            def take_y(n):
                act.wait_ge(y_done, n + 1)
                act.wait_ge(y_free, n + 1)
                act.activation(y[:, half(n, D)], ps_y[:, half(n, D)], ACT.Copy).then_inc(y_taken, 1)

            def tiles(first, end):
                with act.Fori(first, end) as n:
                    gate(n)
                    x_part(n + 2)
                    h_part(n)
                    take_y(n)

            def rest(j, r, more):
                q = 2 * j + r
                first = act.value_load(ends[0:1, bass.ds(q - 1, 1)], min_val=NT, max_val=TILES_MAX - 1)
                end = act.value_load(ends[0:1, bass.ds(q, 1)], min_val=NT + 1, max_val=TILES_MAX)
                tiles(first, end)
                if more:
                    act.wait_ge(raw_ready, q + 2)
                    act.wait_ge(y_done, first + 2)
                    high(q + 3, w_raw[1 - r])

            act.sem_inc(w_high, 2)
            x_part(0)
            x_part(1)
            gate(0)
            x_part(2)
            gate(1)
            x_part(3)
            h_part(1)
            tiles(2, NT // 2)
            act.wait_ge(w_in[0], 16)
            high(2, w_raw[0])
            tiles(NT // 2, NT)
            act.wait_ge(w_in[1], 16)
            high(3, w_raw[1])
            rest(0, 1, True)
            with act.Fori(1, NQ // 2 - 1) as j:
                for r in range(2):
                    rest(j, r, True)
            for r in range(2):
                rest(NQ // 2 - 1, r, False)
            last = last_pair(act)
            tiles(act.value_load(ends[0:1, E - 1:E], min_val=NT, max_val=TILES_MAX - 1), 2 * last + 2)
            h_part(2 * last + 2)
            take_y(2 * last + 2)
            take_y(2 * last + 3)

        @block.vector
        def _(dve):
            dve.sem_inc(x_low, 2)
            dve.sem_inc(clipped, 2)
            dve.sem_inc(h_done, 2)
            dve.sem_inc(h_low, 2)

            def x_part(n, p):
                dve.wait_ge(x_high, n + 1)
                at = slice(p * D, (p + 1) * D)
                dve.tensor_tensor(xT_lo[:, at], ps_x[:, at], f32(xT_hi[:, at]), ALU.subtract).then_inc(x_low, 1)

            def gated_product(n, p):
                dve.wait_ge(gu_done, n + 3)
                dve.wait_ge(h_done, n + 1)
                both = slice(p * 2 * I, (p + 1) * 2 * I)
                dve.tensor_scalar(gu[:, both], ps_gu[:, both], ALPHA, -ALPHA, ALU.min, ALU.max).then_inc(clipped, 1)
                dve.wait_ge(gated, n + 1)
                dve.wait_ge(hT_done, n + 1)
                at = slice(p * I, (p + 1) * I)
                dve.tensor_tensor(h[:, at], act_g[:, at], gu[:, (2 * p + 1) * I:(2 * p + 2) * I], ALU.mult).then_inc(h_done, 1)

            def h_part(n, p):
                dve.wait_ge(h_high, n + 1)
                at = slice(p * I, (p + 1) * I)
                dve.tensor_tensor(hT_lo[:, at], ps_h[:, p * D:p * D + I], f32(hT_hi[:, at]), ALU.subtract).then_inc(h_low, 1)

            x_part(0, 0)
            x_part(1, 1)
            gated_product(0, 0)
            x_part(2, 0)
            last = last_pair(dve)
            with dve.Fori(0, last) as j:
                for n, p in ((2 * j + 1, 1), (2 * j + 2, 0)):
                    gated_product(n, p)
                    x_part(n + 2, p)
                    h_part(2 * j + (1 - p), 1 - p)
            gated_product(2 * last + 1, 1)
            x_part(2 * last + 3, 1)
            h_part(2 * last, 0)
            h_part(2 * last + 1, 1)

        @block.tensor
        def _(pe):
            for s in (xT_done, gu_done, hT_done, y_done):
                pe.sem_inc(s, 2)

            def turn_x(n, p, j):
                pe.wait_ge(x_in[p], 16 * j + 16)
                pe.wait_ge(x_low, n + 1)
                for c in range(DC):
                    at = slice(p * D + c * P, p * D + (c + 1) * P)
                    tr = pe.transpose(ps_x[:, at], xt[:, at], ident[:])
                tr.then_inc(xT_done, 1)

            def parts(T_hi, T_lo, at, start, size):
                w_at = bass.ds(start, size)
                return split3(T_hi[:, at], T_lo[:, at], w_hi[:, w_at], w_lo[:, w_at])

            def gate_up(n, p, q):
                pe.wait_ge(w_low, q + 1)
                pe.wait_ge(x_low, n + 3)
                pe.wait_ge(clipped, n + 1)
                pairs = []
                for c in range(DC):
                    pairs += parts(xT_hi, xT_lo, slice(p * D + c * P, p * D + (c + 1) * P),
                                   (q % WB) * WCOLS + c * 2 * I, 2 * I)
                product(pe, ps_gu[:, p * 2 * I:(p + 1) * 2 * I], pairs).then_inc(gu_done, 1)

            def turn_h(n, p):
                pe.wait_ge(h_done, n + 3)
                pe.wait_ge(h_low, n + 1)
                for c in range(IC):
                    tr = pe.transpose(ps_h[:, p * D + c * P:p * D + (c + 1) * P],
                                      h[:, p * I + c * P:p * I + (c + 1) * P], ident[:])
                tr.then_inc(hT_done, 1)

            def down(n, p, q):
                pe.wait_ge(h_low, n + 3)
                pe.wait_ge(y_taken, n + 1)
                pairs = []
                for c in range(IC):
                    pairs += parts(hT_hi, hT_lo, slice(p * I + c * P, p * I + (c + 1) * P),
                                   (q % WB) * WCOLS + DOWN0 + c * D, D)
                product(pe, ps_y[:, p * D:(p + 1) * D], pairs).then_inc(y_done, 1)

            def experts_of(j, n):
                word = pe.value_load(tile_expert[0:1, bass.ds(j, 1)], min_val=0, max_val=EBASE ** 4 - 1)
                return [word // EBASE ** t % EBASE for t in range(n)]

            turn_x(0, 0, 0)
            turn_x(1, 1, 0)
            gate_up(0, 0, 0)
            turn_x(2, 0, 1)
            gate_up(1, 1, 0)
            turn_x(3, 1, 1)
            turn_h(0, 0)
            last = last_pair(pe)
            with pe.Fori(0, last) as j:
                q = experts_of(j, 4)
                for t in range(2):
                    gate_up(2 * j + (t + 2), t, q[t + 2])
                    turn_x(2 * j + (t + 4), t, j + 2)
                    turn_h(2 * j + (t + 1), 1 - t)
                    down(2 * j + t, t, q[t])
            q = experts_of(last, 2)
            turn_h(2 * last + 1, 1)
            for t in range(2):
                down(2 * last + t, t, q[t])


def combine(nc, x1_all, ys_shared, ys_rows, slots, score, hot, out):
    with ExitStack() as ctx:
        m = Mem(nc, ctx)
        BUF = 4
        STEPS = TOPK + 5
        yr = [m.sb(f"yr{p}", [P, TOPK, D]) for p in range(BUF)]
        yh = [m.sb(f"yh{p}", [P, D]) for p in range(BUF)]
        z = [m.sb(f"z{p}", [P, D]) for p in range(BUF)]
        stats = m.sb("stats2", [P, BUF, 6])
        mv = m.sb("mv2", [P, BUF, 2])
        std = m.sb("std2", [P, BUF, 1])
        rstd = m.sb("rstd2", [P, BUF, 1])
        shift = m.sb("shift2", [P, BUF, 1])
        eps = m.sb("eps2", [P, 1])
        picked = m.sb("picked2", [P, NT, TOPK, E])
        shares = m.sb("shares", [P, NT, TOPK])
        total = m.sb("total", [P, NT, 1])
        gathered = [m.sem(f"gathered{p}") for p in range(BUF)]
        shared_in = [m.sem(f"shared_in{p}") for p in range(BUF)]
        z_out = [m.sem(f"z_out{p}") for p in range(BUF)]
        const = m.sem("const2")
        share = m.sem("share")
        step = [m.sem(f"combine_step{u}") for u in range(2)]
        std_done = m.sem("std2_done")
        scaled = m.sem("scaled")
        block = ctx.enter_context(nc.Block("combine"))
        rows = lambda d, t: d[t * P:(t + 1) * P, :]

        @block.sync
        def _(sp):
            for t in range(BUF):
                sp.dma_start(yh[t][:], rows(ys_shared, t)).then_inc(shared_in[t], 16)
            for t in range(NT):
                p = t % BUF
                sp.wait_ge(scaled, t + 1)
                sp.dma_start(rows(out, t), z[p][:]).then_inc(z_out[p], 16)
                if t + BUF < NT:
                    sp.dma_start(yh[p][:], rows(ys_shared, t + BUF)).then_inc(shared_in[p], 16)
            for p in range(BUF):
                sp.wait_ge(z_out[p], 16 * (NT // BUF))

        @block.gpsimd
        def _(pool):
            for t in range(NT):
                p, u = t % BUF, t % 2
                if t >= BUF:
                    pool.wait_ge(step[u], STEPS * ((t - BUF) // 2) + 1 + TOPK)
                for k in range(TOPK):
                    pool.indirect_dma_start(yr[p][:, k, :], None, ys_rows,
                                            bass.IndirectOffsetOnAxis(ap=slots[:, t, k:k + 1], axis=0)).then_inc(gathered[p], 16)

        @block.scalar
        def _(act):
            act.wait_ge(const, 1)
            for i in range(NT // 2):
                for u in range(2):
                    p = (2 * i + u) % BUF
                    act.wait_ge(step[u], STEPS * i + TOPK + 3)
                    act.activation(std[:, p], mv[:, p, 1:2], ACT.Sqrt, bias=eps[:]).then_inc(std_done, 1)
                for u in range(2):
                    p = (2 * i + u) % BUF
                    act.wait_ge(step[u], STEPS * i + TOPK + 5)
                    act.activation(z[p][:], z[p][:], ACT.Identity, bias=shift[:, p], scale=rstd[:, p]).then_inc(scaled, 1)

        @block.vector
        def _(dve):
            dve.memset(eps[:], EPS).then_inc(const, 1)
            dve.tensor_tensor(picked[:], hot[:], score[:].rearrange("p t (o e) -> p t o e", o=1).to_broadcast([P, NT, TOPK, E]),
                              ALU.mult).then_inc(share, 1)
            dve.wait_ge(share, 1)
            dve.tensor_reduce(shares[:], picked[:], AX.X, ALU.add).then_inc(share, 1)
            dve.wait_ge(share, 2)
            dve.tensor_reduce(total[:, :, 0], shares[:], AX.X, ALU.add).then_inc(share, 1)
            dve.wait_ge(share, 3)
            dve.tensor_scalar(total[:], total[:], 1e-20, None, ALU.add).then_inc(share, 1)
            dve.wait_ge(share, 4)
            dve.reciprocal(total[:], total[:]).then_inc(share, 1)
            dve.wait_ge(share, 5)
            dve.tensor_tensor(shares[:], shares[:], total[:].to_broadcast([P, NT, TOPK]), ALU.mult).then_inc(share, 1)
            dve.wait_ge(share, 6)
            for i in range(NT // 2):
                n = STEPS * i
                both = [(u, 2 * i + u, (2 * i + u) % BUF) for u in range(2)]
                for u, t, p in both:
                    if t >= BUF:
                        dve.wait_ge(z_out[p], 16 * (t // BUF))
                    dve.wait_ge(shared_in[p], 16 * (t // BUF) + 16)
                    dve.tensor_tensor(z[p][:], x1_all[:, t, :], yh[p][:], ALU.add).then_inc(step[u], 1)
                for k in range(TOPK):
                    for u, t, p in both:
                        if k == 0:
                            dve.wait_ge(gathered[p], 16 * TOPK * (t // BUF + 1))
                        dve.wait_ge(step[u], n + 1 + k)
                        dve.scalar_tensor_tensor(z[p][:], yr[p][:, k, :], shares[:, t, k:k + 1], z[p][:],
                                                 ALU.mult, ALU.add).then_inc(step[u], 1)
                for u, t, p in both:
                    dve.wait_ge(step[u], n + TOPK + 1)
                    dve.bn_stats(stats[:, p], z[p][:]).then_inc(step[u], 1)
                for u, t, p in both:
                    dve.wait_ge(step[u], n + TOPK + 2)
                    dve.bn_aggr(mv[:, p], stats[:, p]).then_inc(step[u], 1)
                for u, t, p in both:
                    dve.wait_ge(std_done, t + 1)
                    dve.reciprocal(rstd[:, p], std[:, p]).then_inc(step[u], 1)
                for u, t, p in both:
                    dve.wait_ge(step[u], n + TOPK + 4)
                    dve.scalar_tensor_tensor(shift[:, p], mv[:, p, 0:1], -1.0, rstd[:, p], ALU.mult, ALU.mult).then_inc(step[u], 1)


def build(nc, xT, x, w_qkv, w_out, router_wT, bias, weights, out):
    dram = lambda name, shape: nc.dram_tensor(name, shape, F32, kind="Internal").ap()
    q_hi, q_lo, k_hi, k_lo = (dram(n, (B * D, S)) for n in ("q_hi", "q_lo", "k_hi", "k_lo"))
    attn_T, den, rden = dram("attn_T", (B * D, S)), dram("den", (NH, S)), dram("rden", (NH, S))
    xs, ys = dram("xs", ((TILES_MAX + 2) * P, D)), dram("ys", ((TILES_MAX + 2) * P, D))
    with ExitStack() as ctx:
        v_all = ctx.enter_context(nc.sbuf_tensor("v_all", [P, KB, NH, HD], F32))
        project(nc, xT, w_qkv, q_hi, q_lo, k_hi, k_lo, v_all)
        attend(nc, q_hi, q_lo, k_hi, k_lo, v_all, attn_T, den, xs[T:, :])
    with ExitStack() as ctx:
        m = Mem(nc, ctx)
        ident = m.sb("ident", [P, P])
        x1_all = m.sb("x1_all", [P, NT, D])
        logits = m.sb("logits", [P, NT, E])
        slots = m.sb("slots", [P, NT, TOPK], U32)
        score = m.sb("score", [P, NT, E])
        hot = m.sb("hot", [P, NT, TOPK, E])
        tile_expert = m.sb("tile_expert", [1, TILES_MAX // 2], I32)
        ends = m.sb("ends", [1, E + 3], I32)
        made = m.sem("ident_made")
        with nc.Block("identity") as block:
            @block.gpsimd
            def _(pool):
                pool.memset(ident[:], 0.0).then_inc(made, 1)
                pool.wait_ge(made, 1)
                pool.affine_select(out=ident[:], in_=ident[:], compare_op=ALU.not_equal, fill=1.0, base=0,
                                   pattern=[[-1, P]], channel_multiplier=1).then_inc(made, 1)
        mix(nc, attn_T, den, rden, w_out, x, router_wT, ident, x1_all, logits)
        with ExitStack() as inner:
            bufs = ExpertBuffers(Mem(nc, inner))
            route(nc, ident, x1_all, logits, bias, xs[0:T, :], slots, score, hot, tile_expert, ends, weights, bufs)
            experts(nc, weights, bufs, x1_all, slots, xs, ys, ident, tile_expert, ends)
        combine(nc, x1_all, ys[0:T, :], ys, slots, score, hot, out)


def lay_out(gate, up, down):
    n = gate.shape[0]
    gu = np.concatenate([gate.transpose(0, 2, 1), up.transpose(0, 2, 1)], axis=2)
    gu = gu.reshape(n, DC, P, 2 * I).transpose(2, 0, 1, 3).reshape(P, n, DOWN0)
    dn = down.transpose(0, 2, 1).reshape(n, IC, P, D).transpose(2, 0, 1, 3).reshape(P, n, IC * D)
    return np.ascontiguousarray(np.concatenate([gu, dn], axis=2).reshape(P, n * WCOLS))


def kernel(L0_attn_x, L0_attn_w_qkv, L0_attn_w_out, L0_ffn_router_w, L0_ffn_expert_bias, L0_ffn_gate_w, L0_ffn_up_w,
           L0_ffn_down_w, L0_ffn_shared_gate_w, L0_ffn_shared_up_w, L0_ffn_shared_down_w):
    import concourse.bacc as _bacc
    from concourse.bass_utils import run_bass_kernel_spmd as _run

    x = np.asarray(L0_attn_x).reshape(T, D)
    stack = lambda shared, others: np.concatenate([np.asarray(shared)[None], np.asarray(others)])
    arrays = dict(
        xT=x.T, x=x, w_qkv=np.asarray(L0_attn_w_qkv), w_out=np.asarray(L0_attn_w_out),
        router_wT=np.asarray(L0_ffn_router_w).T, bias=np.asarray(L0_ffn_expert_bias).reshape(1, E),
        weights=lay_out(stack(L0_ffn_shared_gate_w, L0_ffn_gate_w), stack(L0_ffn_shared_up_w, L0_ffn_up_w),
                        stack(L0_ffn_shared_down_w, L0_ffn_down_w)))
    arrays = {f"in_{name}_dram": np.ascontiguousarray(a) for name, a in arrays.items()}
    nc = _bacc.Bacc("TRN2", target_bir_lowering=False, num_devices=1)
    args = [nc.dram_tensor(name, a.shape, F32, kind="ExternalInput").ap() for name, a in arrays.items()]
    out = nc.dram_tensor("out_0_dram", (T, D), F32, kind="ExternalOutput").ap()
    build(nc, *args, out)
    result = _run(nc, [arrays], core_ids=[0])
    return result.results[0]["out_0_dram"].reshape(B, S, D)
```
